# Optimizing a Trainium2 kernel written in Bass

```python
import numpy as np
import jax
import jax.numpy as jnp

def _softmax(x, axis=-1):
    return jax.nn.softmax(x, axis=axis)

def _gelu(x):
    return jax.nn.gelu(x, approximate=True)

def _silu(x):
    return jax.nn.silu(x)

def _sigmoid(x):
    return jax.nn.sigmoid(x)

def _layernorm(x, axis=-1, eps=1e-05):
    m = jnp.mean(x, axis=axis, keepdims=True)
    v = jnp.var(x, axis=axis, keepdims=True)
    return (x - m) / jnp.sqrt(v + eps)

def _scatter_add(tgt, idx, src, axis=0):
    return tgt.at[idx].add(src)

def _segment_sum(src, seg, n):
    return jax.ops.segment_sum(src, seg, n)
kernel_name = 'mk_seq_postln_d1_jaxref_r8_1ed4a5'

def setup_inputs(seed: int=0):
    np.random.seed(seed)
    _w = jnp.asarray

    def _L0_attn_setup():
        import jax, jax.numpy as jnp
        import numpy as np
        BATCH, SEQ, D_MODEL, STATE_DIM = (8, 256, 128, 128)

        def _cayley_circulant_eigenvalues(a_params, n):
            half_n = n // 2
            a_full = jnp.zeros((n,), dtype=a_params.dtype)
            a_full = a_full.at[1:half_n].set(a_params[:half_n - 1])
            a_full = a_full.at[half_n + 1:].set(-a_params[:half_n - 1][::-1])
            omega = jnp.fft.fft(a_full).imag
            w2 = omega * omega
            denom = 1.0 + w2
            return ((1.0 - w2) / denom + 1j * (-2.0 * omega / denom)).astype(jnp.complex64)
        key = jax.random.key(seed)
        k1, k2, k3, k4 = jax.random.split(key, 4)
        u = jax.random.normal(k1, (BATCH, SEQ, D_MODEL), dtype=jnp.float32)
        a_params = jax.random.normal(k2, (STATE_DIM // 2,), dtype=jnp.float32) * 0.1
        B_w = jax.random.normal(k3, (STATE_DIM, D_MODEL), dtype=jnp.float32) / np.sqrt(D_MODEL).astype(np.float32)
        C_w = jax.random.normal(k4, (D_MODEL, STATE_DIM), dtype=jnp.float32) / np.sqrt(STATE_DIM).astype(np.float32)
        D = jnp.zeros((D_MODEL,), dtype=jnp.float32)
        return {'u': u, 'a_params': a_params, 'B_w': B_w, 'C_w': C_w, 'D': D}
    _L0_attn_in = _L0_attn_setup()

    def _L0_ffn_setup():
        import jax, jax.numpy as jnp
        import numpy as np
        D = 128
        H = 256
        E = 8
        TOP_K = 2
        N_SHARED = 1
        B, S = (2, 128)
        key = jax.random.key(seed)
        ks = jax.random.split(key, 12)
        sc = 0.02
        return {'hidden': jax.random.normal(ks[0], (B, S, D), jnp.float32), 'router_w': jax.random.normal(ks[1], (D, E), jnp.float32) * sc, 'router_b': jnp.zeros((E,), jnp.float32), 'sw1': jax.random.normal(ks[2], (D, H), jnp.float32) * sc, 'sb1': jnp.zeros((H,), jnp.float32), 'sw2': jax.random.normal(ks[3], (H, D), jnp.float32) * sc, 'sb2': jnp.zeros((D,), jnp.float32), 'rw1': jax.random.normal(ks[4], (E, D, H), jnp.float32) * sc, 'rb1': jnp.zeros((E, H), jnp.float32), 'rw2': jax.random.normal(ks[5], (E, H, D), jnp.float32) * sc, 'rb2': jnp.zeros((E, D), jnp.float32)}
    _L0_ffn_in = _L0_ffn_setup()
    _d = {'L0_attn_u': _L0_attn_in['u'], 'L0_attn_a_params': _L0_attn_in['a_params'], 'L0_attn_B_w': _L0_attn_in['B_w'], 'L0_attn_C_w': _L0_attn_in['C_w'], 'L0_attn_D': _L0_attn_in['D'], 'L0_ffn_router_w': _L0_ffn_in['router_w'], 'L0_ffn_router_b': _L0_ffn_in['router_b'], 'L0_ffn_sw1': _L0_ffn_in['sw1'], 'L0_ffn_sb1': _L0_ffn_in['sb1'], 'L0_ffn_sw2': _L0_ffn_in['sw2'], 'L0_ffn_sb2': _L0_ffn_in['sb2'], 'L0_ffn_rw1': _L0_ffn_in['rw1'], 'L0_ffn_rb1': _L0_ffn_in['rb1'], 'L0_ffn_rw2': _L0_ffn_in['rw2'], 'L0_ffn_rb2': _L0_ffn_in['rb2']}
    _x0 = _d['L0_attn_u']
    _d['L0_attn_u'] = jax.random.normal(jax.random.fold_in(jax.random.key(seed), 1), (32, 256, 128), dtype=_x0.dtype)
    del _x0
    return _d

def reference(L0_attn_u, L0_attn_a_params, L0_attn_B_w, L0_attn_C_w, L0_attn_D, L0_ffn_router_w, L0_ffn_router_b, L0_ffn_sw1, L0_ffn_sb1, L0_ffn_sw2, L0_ffn_sb2, L0_ffn_rw1, L0_ffn_rb1, L0_ffn_rw2, L0_ffn_rb2):

    def _L0_attn_ref(u, a_params, B_w, C_w, D):
        import jax, jax.numpy as jnp
        import numpy as np
        BATCH, SEQ, D_MODEL, STATE_DIM = (8, 256, 128, 128)

        def _cayley_circulant_eigenvalues(a_params, n):
            half_n = n // 2
            a_full = jnp.zeros((n,), dtype=a_params.dtype)
            a_full = a_full.at[1:half_n].set(a_params[:half_n - 1])
            a_full = a_full.at[half_n + 1:].set(-a_params[:half_n - 1][::-1])
            omega = jnp.fft.fft(a_full).imag
            w2 = omega * omega
            denom = 1.0 + w2
            return ((1.0 - w2) / denom + 1j * (-2.0 * omega / denom)).astype(jnp.complex64)
        n = B_w.shape[0]
        lambdas = _cayley_circulant_eigenvalues(a_params, n)
        Bu = jnp.einsum('bsd,nd->bsn', u, B_w)

        def step(h, bu_t):
            Wh = jnp.fft.ifft(lambdas * jnp.fft.fft(h.astype(jnp.float32))).real.astype(h.dtype)
            h_new = Wh + bu_t
            return (h_new, h_new)
        h0 = jnp.zeros((u.shape[0], n), dtype=u.dtype)
        _, hs = jax.lax.scan(step, h0, jnp.swapaxes(Bu, 0, 1))
        y = jnp.einsum('sbn,dn->bsd', hs, C_w) + D * u
        return y

    def _L0_ffn_ref(hidden, router_w, router_b, sw1, sb1, sw2, sb2, rw1, rb1, rw2, rb2):
        import jax, jax.numpy as jnp
        import numpy as np
        D = 128
        H = 256
        E = 8
        TOP_K = 2
        N_SHARED = 1
        B, S = (2, 128)
        b, s, d = hidden.shape
        T = b * s
        flat = hidden.reshape(T, d)
        router_logits = flat @ router_w + router_b
        router_probs = jax.nn.softmax(router_logits, axis=-1)
        topk_probs, topk_idx = jax.lax.top_k(router_probs, TOP_K)
        weights = jnp.zeros_like(router_probs).at[jnp.arange(T)[:, None], topk_idx].add(topk_probs)
        sh = jax.nn.gelu(flat @ sw1 + sb1, approximate=False)
        shared_out = (sh @ sw2 + sb2) / N_SHARED
        h1 = jax.nn.gelu(jnp.einsum('td,edh->teh', flat, rw1) + rb1[None], approximate=False)
        expert_out = jnp.einsum('teh,ehd->ted', h1, rw2) + rb2[None]
        mixed = jnp.einsum('ted,te->td', expert_out, weights)
        return (shared_out + mixed).reshape(b, s, d)
    x = L0_attn_u
    x = _layernorm(x + _L0_attn_ref(x, L0_attn_a_params, L0_attn_B_w, L0_attn_C_w, L0_attn_D), axis=-1)
    x = _layernorm(x + _L0_ffn_ref(x, L0_ffn_router_w, L0_ffn_router_b, L0_ffn_sw1, L0_ffn_sb1, L0_ffn_sw2, L0_ffn_sb2, L0_ffn_rw1, L0_ffn_rb1, L0_ffn_rw2, L0_ffn_rb2), axis=-1)
    return x

_drawn_inputs = setup_inputs


def setup_inputs(seed=0):
    import zlib

    import numpy as np

    out = dict(_drawn_inputs(seed))
    spreads = {'L0_attn_D': (0.0, 0.601),
     'L0_ffn_router_b': (0.0, 0.627),
     'L0_ffn_sb1': (0.0, 0.513),
     'L0_ffn_sb2': (0.0, 0.1),
     'L0_ffn_rb1': (0.0, 0.8),
     'L0_ffn_rb2': (0.0, 0.342)}
    factors = {'L0_ffn_rw1': 6.529, 'L0_ffn_rw2': 5.848}
    for name, (base, spread) in spreads.items():
        noise = np.random.default_rng([zlib.crc32(name.encode()), seed]).standard_normal(out[name].shape)
        drawn = base * np.exp(spread * noise) if base else spread * noise
        out[name] = jnp.asarray(drawn.astype(out[name].dtype))
    for name, factor in factors.items():
        out[name] = (out[name] * factor).astype(out[name].dtype)
    return out
```

```python
from contextlib import ExitStack

import numpy as np

import concourse.bass as bass
from concourse import mybir

F32 = mybir.dt.float32
F32R = mybir.dt.float32r
ALU = mybir.AluOpType
ACT = mybir.ActivationFunctionType
AX = mybir.AxisListType.X

P = 128
SEQ = 256
NSEQ = 32
GT = 512
NG = NSEQ * SEQ // GT
TPG = GT // P
SPG = GT // SEQ
E = 8
NX = E + 1
HB = 2
HID = HB * P
EPS = 1e-5
PEEL = 6
LAST = 14


def shape_constants():
    n = np.arange(P)
    p = np.arange(P)
    k = np.where(p <= 64, p, p - 64)
    im = p > 64
    edge = (p == 0) | (p == 64)
    ang = 2 * np.pi * np.outer(n, k) / P
    cos, sin = np.cos(ang), np.sin(ang)
    sin[:, edge] = 0
    to_basis = np.where(im, -sin, cos)
    to_turned = np.where(im, -cos, -sin)
    to_turned[:, edge] = 0
    m = np.where(edge, 1.0, 2.0)
    from_basis = np.where(im, -sin, cos) * m / P
    from_turned = np.where(im, -cos, -sin) * m / P
    from_turned[:, edge] = 0
    omega = np.zeros((P, P))
    omega[:63] = -2 * np.sin(2 * np.pi * np.outer(np.arange(1, 64), k) / P)
    omega[:, edge] = 0
    key = np.tile(E - np.arange(E), (P, 1))
    row01 = np.zeros((P, 2))
    row01[0, 0] = row01[1, 1] = 1
    parts = [to_basis, to_turned, from_basis, from_turned, np.eye(P), omega, key, row01]
    return np.ascontiguousarray(np.concatenate(parts, axis=1).astype(np.float32))


NCONST = 6 * P + E + 2


def build(nc, consts, u, a_params, B_w, C_w, D, router_w, router_b, sw1, sb1, sw2, sb2, rw1, rb1, rw2, rb2, out):
    x_d = u.rearrange("b s d -> (b s) d").rearrange("(g t p) d -> g p t d", p=P, t=TPG)
    out_d = out.rearrange("b s d -> (b s) d").rearrange("(g t p) d -> g p t d", p=P, t=TPG)

    with ExitStack() as ctx:
        def sb(name, shape, dt=F32):
            return ctx.enter_context(nc.sbuf_tensor(name, shape, dt))

        def sem(name):
            return ctx.enter_context(nc.semaphore(name))

        bank = [ctx.enter_context(nc.psum_tensor(f"bank{i}", [P, 512], F32)) for i in range(8)]
        ps_xT, ps_b1, ps_b2, ps_x1T, ps_lg = bank[0], bank[1], bank[2], bank[3], bank[4]
        ps_r = [bank[5], bank[6]]
        ps_h = bank[0:4]
        ps_y = bank[4:8]

        cst = sb("cst", [P, NCONST])
        to_basis, to_turned, from_basis, from_turned, ident, omega_m = (
            cst[:, i * P:(i + 1) * P] for i in range(6))
        first_key = cst[:, 6 * P:6 * P + E]
        row0, row1 = (cst[:, 6 * P + E + i:6 * P + E + i + 1] for i in range(2))
        bw = sb("bw", [P, P])
        cw = sb("cw", [P, P])
        cwT = sb("cwT", [P, P])
        apar = sb("apar", [64, 1])
        dcol = sb("dcol", [P, 1])
        rw = sb("rw", [P, E])
        rw_hi = sb("rw_hi", [P, E], F32R)
        rw_lo = sb("rw_lo", [P, E], F32R)
        rbias = sb("rbias", [P, E])
        g1T = sb("g1T", [P, P])
        g2T = sb("g2T", [P, P])
        m1T = sb("m1T", [P, P])
        m2T = sb("m2T", [P, P])
        skip = sb("skip", [P, P])
        lam = sb("lam", [P, 8])
        cosT = sb("cosT", [P, SEQ])
        sinT = sb("sinT", [P, SEQ])
        tmpT = sb("tmpT", [P, 2, SEQ // 2])

        w1f = sb("w1f", [P, NX, HID])
        w1_hi = sb("w1_hi", [P, NX, HID], F32R)
        w1_lo = sb("w1_lo", [P, NX, HID], F32R)
        w2 = sb("w2", [P, NX, HB, P])
        b1r = sb("b1r", [NX * HB, P])
        b1c = sb("b1c", [P, NX * HB])
        b2f = sb("b2f", [2, NX, P])
        b2h = sb("b2h", [2, NX, P])
        b2l = sb("b2l", [2, NX, P])
        b2 = sb("b2", [2, NX, P], F32R)
        ones2 = sb("ones2", [2, P], F32R)
        onesf = sb("onesf", [2, P])

        xg = [sb(f"xg{i}", [P, TPG, P]) for i in range(2)]
        uT = [sb(f"uT{i}", [P, GT]) for i in range(2)]
        z1 = sb("z1", [P, GT])
        z2 = sb("z2", [P, GT])
        run = sb("run", [P, GT])
        h = [sb(f"h{i}", [P, HB, GT]) for i in range(2)]
        hc = [h[i][:, 0, :] for i in range(2)]
        hs = [h[i][:, 1, :] for i in range(2)]
        st = sb("st", [P, TPG, 6])
        mt = sb("mt", [P, 3, TPG])
        mean = sb("mean", [P, TPG])
        veps = sb("veps", [P, TPG])
        lnv = sb("lnv", [P, TPG])
        rs0 = sb("rs0", [P, TPG])
        nt = sb("nt", [P, 4, TPG])
        rstd = sb("rstd", [P, TPG])
        lg = sb("lg", [P, TPG, E])
        lgs = sb("lgs", [P, TPG, E])
        ex = sb("ex", [P, TPG, E])
        pr = sb("pr", [P, TPG, E])
        pr2 = sb("pr2", [P, TPG, E])
        rt = sb("rt", [P, 4, TPG, E])
        rc = sb("rc", [P, 8, TPG])

        x1b = [sb(f"x1b{i}", [P, TPG, P]) for i in range(2)]
        xr_hi = [sb(f"xr_hi{i}", [P, GT], F32R) for i in range(2)]
        xr_lo = [sb(f"xr_lo{i}", [P, GT], F32R) for i in range(2)]

        X1 = sb("X1", [P, NG * TPG, P])
        x1_hi = sb("x1_hi", [P, NG * GT], F32R)
        x1_lo = sb("x1_lo", [P, NG * GT], F32R)
        wt = sb("wt", [P, NG * TPG, E])

        sta2 = sb("sta2", [P, NG * TPG, 6])
        mean2 = sb("mean2", [P, NG * TPG])
        veps2 = sb("veps2", [P, NG * TPG])
        lnv2 = sb("lnv2", [P, NG * TPG])
        rs02 = sb("rs02", [P, NG * TPG])
        nt2 = sb("nt2", [P, 3, NG * TPG])
        rstd2 = sb("rstd2", [P, NG * TPG])

        s_small = sem("s_small")
        s_wload = sem("s_wload")
        x_in = [sem(f"x_in{i}") for i in range(2)]
        x1_kept = [sem(f"x1_kept{i}") for i in range(2)]
        hi_kept = [sem(f"hi_kept{i}") for i in range(2)]
        lo_kept = [sem(f"lo_kept{i}") for i in range(2)]
        w_parts = sem("w_parts")
        set_pe = sem("set_pe")
        set_act = sem("set_act")
        set_dve = sem("set_dve")
        tab = sem("tab")
        xT_ps = sem("xT_ps")
        uT_sb = sem("uT_sb")
        b_ps = sem("b_ps")
        z_sb = sem("z_sb")
        run_sb = sem("run_sb")
        rot_sb = sem("rot_sb")
        r_ps = sem("r_ps")
        stats = sem("stats")
        aggr = sem("aggr")
        veps_sb = sem("veps_sb")
        lnv_sb = sem("lnv_sb")
        rs0_sb = sem("rs0_sb")
        newton = sem("newton")
        x1_sb = sem("x1_sb")
        x1T_ps = sem("x1T_ps")
        hi_sb = sem("hi_sb")
        lo_sb = sem("lo_sb")
        lg_ps = sem("lg_ps")
        lg_sb = sem("lg_sb")
        lgs_sb = sem("lgs_sb")
        lmax = sem("lmax")
        b2_step = sem("b2_step")
        ex_sb = sem("ex_sb")
        rchain = sem("rchain")
        wt_sb = sem("wt_sb")
        h_ps = sem("h_ps")
        h_sb = sem("h_sb")
        y_ps = sem("y_ps")
        acc_sb = sem("acc_sb")
        st2 = sem("st2")
        out_sb = sem("out_sb")
        out_done = sem("out_done")

        block = ctx.enter_context(nc.Block())

        def pipeline(eng, step):
            for i in range(-1, PEEL):
                step(i, i % 2)
            with eng.Fori(PEEL, LAST - 1, 2) as i:
                step(i, 0)
                step(i + 1, 1)
            for i in range(LAST, NG + 3):
                step(i, i % 2)

        def is_first(g):
            return isinstance(g, int) and g == 0

        def group(i, lag):
            g = i - lag
            return g if not isinstance(g, int) or 0 <= g < NG else None

        def reused(eng, s, g, depth, each=1):
            if not isinstance(g, int) or g >= depth:
                eng.wait_ge(s, (g - (depth - 1)) * each)

        def slot_count(g, v):
            return 8 * g + 16 - 8 * v

        def free_slot(eng, s, g, v):
            if not isinstance(g, int) or g >= 2:
                eng.wait_ge(s, slot_count(g - 2, v))

        def tile(a, n):
            return a[:, bass.ds(n, 1), :].rearrange("p o d -> p (o d)")

        @block.sync
        def _(sp):
            small = [(cst[:, :], consts), (bw[:, :], B_w), (cw[:, :], C_w),
                     (apar[:, :], a_params.rearrange("(p o) -> p o", o=1)),
                     (dcol[:, :], D.rearrange("(p o) -> p o", o=1)),
                     (rw[:, :], router_w), (rbias[:, :], router_b.partition_broadcast(P))]
            for dst, src in small:
                sp.dma_start(dst, src).then_inc(s_small, 16)
            for g in range(2):
                sp.dma_start(xg[g][:, :, :], x_d[g]).then_inc(x_in[g], 16)
            big = [(w1f[:, 0:E, :], rw1.rearrange("e d h -> d e h")), (w1f[:, E, :], sw1),
                   (b1r[0:E * HB, :], rb1.rearrange("e (b h) -> (e b) h", b=HB)),
                   (b1r[E * HB:, :], sb1.rearrange("(b h) -> b h", b=HB)),
                   (b2f[0:1, 0:E, :], rb2.unsqueeze(0)), (b2f[1:2, 0:E, :], rb2.unsqueeze(0)),
                   (b2f[0:1, E, :], sb2.unsqueeze(0)), (b2f[1:2, E, :], sb2.unsqueeze(0)),
                   (w2[:, E, :, :], sw2.rearrange("(b h) d -> h b d", b=HB))]
            for e in range(E):
                big.append((w2[:, e, :, :], rw2[e].rearrange("(b h) d -> h b d", b=HB)))
            for dst, src in big:
                sp.dma_start(dst, src).then_inc(s_wload, 16)
            def keep(g, v):
                sp.wait_ge(x1_sb, g + 1)
                sp.dma_start(X1[:, bass.ds(g * TPG, TPG), :], x1b[v][:, :, :]).then_inc(x1_kept[v], 16)
                sp.wait_ge(lo_sb, g + 1)
                sp.wait_ge(hi_sb, g + 1)
                sp.dma_start(x1_hi[:, bass.ds(g * GT, GT)].bitcast(F32), xr_hi[v][:, :].bitcast(F32)).then_inc(hi_kept[v], 16)
                sp.dma_start(x1_lo[:, bass.ds(g * GT, GT)].bitcast(F32), xr_lo[v][:, :].bitcast(F32)).then_inc(lo_kept[v], 16)

            with sp.Fori(0, NG - 3, 2) as g:
                for v in range(2):
                    sp.wait_ge(xT_ps, g + v + 1)
                    sp.dma_start(xg[v][:, :, :], x_d[bass.ds(g + v + 2, 1)].rearrange("o p t d -> (o p) t d")).then_inc(x_in[v], 16)
                    keep(g + v, v)
            for g in range(NG - 2, NG):
                keep(g, g % 2)
            with sp.Fori(0, NG) as g:
                sp.wait_ge(out_sb, g + 1)
                sp.dma_start(out_d[bass.ds(g, 1)].rearrange("o p t d -> (o p) t d"), X1[:, bass.ds(g * TPG, TPG), :]).then_inc(out_done, 16)
            sp.wait_ge(out_done, NG * 16)

        @block.tensor
        def _(pe):
            mm = pe.matmul
            pe.wait_ge(s_small, 7 * 16)
            mm(ps_b1[:, 0:1], omega_m[0:63, :], apar[0:63, :], start=True, stop=True).then_inc(set_pe, 1)
            mm(ps_b2[:, 0:P], bw[:, :], to_basis, start=True, stop=True)
            mm(ps_b2[:, P:2 * P], bw[:, :], to_turned, start=True, stop=True)
            pe.transpose(ps_b2[:, 2 * P:3 * P], cw[:, :], ident).then_inc(set_pe, 1)
            pe.wait_ge(set_act, 1)
            mm(ps_x1T[:, 0:P], from_basis, cwT[:, :], start=True, stop=True)
            mm(ps_x1T[:, P:2 * P], from_turned, cwT[:, :], start=True, stop=True).then_inc(set_pe, 1)
            pe.wait_ge(s_wload, 17 * 16)
            pe.transpose(ps_lg[:, 0:NX * HB], b1r[:, :], ident[0:NX * HB, 0:NX * HB]).then_inc(set_pe, 1)

            def step(i, v):
                g = group(i, 1)
                if g is not None:
                    w = 1 - v
                    pe.wait_ge(rot_sb, g + 1)
                    if is_first(g):
                        pe.wait_ge(set_act, 3)
                        pe.wait_ge(set_dve, 1)
                    reused(pe, x1_sb, g, 2)
                    for t in range(TPG):
                        c = slice(t * P, (t + 1) * P)
                        mm(ps_r[w][:, c], hc[w][:, c], m1T[:, :], start=True, stop=False)
                        mm(ps_r[w][:, c], hs[w][:, c], m2T[:, :], start=False, stop=False)
                        last = mm(ps_r[w][:, c], uT[w][:, c], skip[:, :], start=False, stop=True)
                    last.then_inc(r_ps, 1)
                g = group(i, 3)
                if g is not None:
                    pe.wait_ge(hi_sb, g + 1)
                    pe.wait_ge(lo_sb, g + 1)
                    if is_first(g):
                        pe.wait_ge(set_act, 4)
                        pe.wait_ge(w_parts, 2)
                    reused(pe, lg_sb, g, 1)
                    w = 1 - v
                    for t in range(TPG):
                        c = slice(t * P, (t + 1) * P)
                        o = ps_lg[:, t * E:(t + 1) * E]
                        mm(o, xr_hi[w][:, c], rw_hi[:, :], start=True, stop=False)
                        mm(o, xr_hi[w][:, c], rw_lo[:, :], start=False, stop=False)
                        last = mm(o, xr_lo[w][:, c], rw_hi[:, :], start=False, stop=True)
                    last.then_inc(lg_ps, 1)
                g = group(i, 0)
                if g is not None:
                    pe.wait_ge(uT_sb, g + 1)
                    if is_first(g):
                        pe.wait_ge(set_act, 2)
                        pe.wait_ge(tab, 2)
                    reused(pe, z_sb, g, 1)
                    mm(ps_b1[:, :], g1T[:, :], uT[v][:, :], start=True, stop=True)
                    mm(ps_b2[:, :], g2T[:, :], uT[v][:, :], start=True, stop=True).then_inc(b_ps, 1)
                g = group(i, 2)
                if g is not None:
                    pe.wait_ge(x1_sb, g + 1)
                    if is_first(g):
                        pe.wait_ge(set_act, 3)
                    reused(pe, lo_sb, g, 1)
                    reused(pe, hi_sb, g, 1)
                    for t in range(TPG):
                        last = pe.transpose(ps_x1T[:, t * P:(t + 1) * P], x1b[v][:, t, :], ident)
                    last.then_inc(x1T_ps, 1)
                g = group(i, -1)
                if g is not None:
                    w = 1 - v
                    pe.wait_ge(x_in[w], slot_count(g, w))
                    reused(pe, uT_sb, g, 1)
                    for t in range(TPG):
                        last = pe.transpose(ps_xT[:, t * P:(t + 1) * P], xg[w][:, t, :], ident)
                    last.then_inc(xT_ps, 1)

            pipeline(pe, step)

            for s in (uT_sb, z_sb, x1_sb, hi_sb, lo_sb, lg_sb):
                pe.wait_ge(s, NG)
            for v in range(2):
                pe.wait_ge(hi_kept[v], NG * 8)
                pe.wait_ge(lo_kept[v], NG * 8)
            pe.wait_ge(w_parts, 7)

            def first_layer(g, n, k, e):
                if not isinstance(n, int) or n >= 2:
                    pe.wait_ge(h_sb, 2 * n - 2)
                xh, xl = (a[:, bass.ds(g * GT, GT)] for a in (x1_hi, x1_lo))
                for b in range(HB):
                    o = ps_h[2 * k + b][:, :]
                    c = slice(b * P, (b + 1) * P)
                    mm(o, w1_hi[:, e, c], xh, start=True, stop=False)
                    mm(o, w1_lo[:, e, c], xh, start=False, stop=False)
                    mm(o, w1_hi[:, e, c], xl, start=False, stop=True).then_inc(h_ps, 1)

            def second_layer(n, k, e):
                pe.wait_ge(h_sb, 2 * n + 2)
                if not isinstance(n, int) or n >= 2:
                    pe.wait_ge(acc_sb, n - 1)
                for t in range(TPG):
                    c = slice(t * P, (t + 1) * P)
                    o = ps_y[k][:, c]
                    mm(o, ones2[:, :], b2[:, e, :], start=True, stop=False)
                    for b in range(HB):
                        last = mm(o, h[k][:, b, c], w2[:, e, b, :], start=False, stop=b == HB - 1)
                last.then_inc(y_ps, 1)

            ORDER = [E] + list(range(E))
            first_layer(0, 0, 0, E)
            for m in range(1, 2 * NX):
                first_layer(m // NX, m, m % 2, ORDER[m % NX])
                second_layer(m - 1, (m - 1) % 2, ORDER[(m - 1) % NX])
            with pe.Fori(2, NG - 1, 2) as g:
                for m in range(2 * NX):
                    first_layer(g + m // NX, g * NX + m, m % 2, ORDER[m % NX])
                    second_layer(g * NX + (m - 1), (m - 1) % 2, ORDER[(m - 1) % NX])
            second_layer(NG * NX - 1, (NG * NX - 1) % 2, ORDER[-1])

        @block.gpsimd
        def _(pool):
            pool.wait_ge(s_small, 7 * 16)
            pool.tensor_copy(rw_hi[:, :], rw[:, :]).then_inc(w_parts, 1)
            pool.wait_ge(w_parts, 1)
            pool.tensor_tensor(rw_lo[:, :], rw[:, :], rw_hi[:, :].bitcast(F32), ALU.subtract).then_inc(w_parts, 1)
            pool.memset(onesf[:, :], 1.0).then_inc(w_parts, 1)
            pool.wait_ge(s_wload, 17 * 16)
            pool.tensor_copy(w1_hi[:, :, :], w1f[:, :, :]).then_inc(w_parts, 1)
            pool.wait_ge(w_parts, 4)
            pool.tensor_copy(ones2[:, :], onesf[:, :])
            pool.tensor_tensor(w1_lo[:, :, :], w1f[:, :, :], w1_hi[:, :, :].bitcast(F32), ALU.subtract).then_inc(w_parts, 1)
            pool.tensor_copy(b2h[:, :, :].bitcast(F32R), b2f[:, :, :]).then_inc(w_parts, 1)
            pool.wait_ge(w_parts, 6)
            pool.tensor_tensor(b2l[:, :, :], b2f[:, :, :], b2h[:, :, :], ALU.subtract).then_inc(b2_step, 1)
            pool.wait_ge(b2_step, 1)
            pool.tensor_scalar(b2l[:, :, :], b2l[:, :, :], row1[0:2, :], None, ALU.mult).then_inc(b2_step, 1)
            pool.tensor_scalar(b2h[:, :, :], b2h[:, :, :], row0[0:2, :], None, ALU.mult).then_inc(b2_step, 1)
            pool.wait_ge(b2_step, 3)
            pool.tensor_tensor(b2[:, :, :], b2h[:, :, :], b2l[:, :, :], ALU.add).then_inc(w_parts, 1)

        @block.scalar
        def _(act):
            act.wait_ge(set_pe, 2)
            act.copy(cwT[:, :], ps_b2[:, 2 * P:3 * P]).then_inc(set_act, 1)
            act.copy(g1T[:, :], ps_b2[:, 0:P])
            act.copy(g2T[:, :], ps_b2[:, P:2 * P]).then_inc(set_act, 1)
            act.wait_ge(set_pe, 3)
            act.copy(m1T[:, :], ps_x1T[:, 0:P])
            act.copy(m2T[:, :], ps_x1T[:, P:2 * P]).then_inc(set_act, 1)
            act.wait_ge(set_pe, 4)
            act.copy(b1c[:, :], ps_lg[:, 0:NX * HB]).then_inc(set_act, 1)

            def step(i, v):
                g = group(i, 1)
                if g is not None:
                    act.wait_ge(veps_sb, g + 1)
                    act.activation(lnv[:, :], veps[:, :], ACT.Ln).then_inc(lnv_sb, 1)
                    act.wait_ge(lnv_sb, g + 1)
                    reused(act, x1_sb, g, 1)
                    act.activation(rs0[:, :], lnv[:, :], ACT.Exp, scale=-0.5).then_inc(rs0_sb, 1)
                g = group(i, 3)
                if g is not None:
                    act.wait_ge(lgs_sb, g + 1)
                    reused(act, wt_sb, g, 1)
                    act.activation(ex[:, :, :], lgs[:, :, :], ACT.Exp).then_inc(ex_sb, 1)
                g = group(i, 2)
                if g is not None:
                    act.wait_ge(x1T_ps, g + 1)
                    reused(act, lg_ps, g, 2)
                    free_slot(act, hi_kept[v], g, v)
                    act.copy(xr_hi[v][:, :], ps_x1T[:, :]).then_inc(hi_sb, 1)
                g = group(i, -1)
                if g is not None:
                    act.wait_ge(xT_ps, g + 1)
                    reused(act, r_ps, g, 2)
                    act.copy(uT[1 - v][:, :], ps_xT[:, :]).then_inc(uT_sb, 1)

            pipeline(act, step)
            act.wait_ge(r_ps, NG)

            def hidden(n, k, e):
                if not isinstance(n, int) or n >= 2:
                    act.wait_ge(y_ps, n - 1)
                for b in range(HB):
                    act.wait_ge(h_ps, 2 * n + b + 1)
                    act.activation(h[k][:, b, :], ps_h[2 * k + b][:, :], ACT.Gelu,
                                   bias=b1c[:, e * HB + b:e * HB + b + 1]).then_inc(h_sb, 1)

            ORDER = [E] + list(range(E))
            for m in range(2 * NX):
                hidden(m, m % 2, ORDER[m % NX])
            with act.Fori(2, NG - 1, 2) as g:
                for m in range(2 * NX):
                    hidden(g * NX + m, m % 2, ORDER[m % NX])

            act.wait_ge(st2, 1)
            act.activation(lnv2[:, :], veps2[:, :], ACT.Ln).then_inc(lnv_sb, 1)
            act.wait_ge(lnv_sb, NG + 1)
            act.activation(rs02[:, :], lnv2[:, :], ACT.Exp, scale=-0.5).then_inc(rs0_sb, 1)

        @block.vector
        def _(dve):
            def linker(s):
                n = [0]

                def link(base, ins):
                    n[0] += 1
                    ins.then_inc(s, 1)
                    dve.wait_ge(s, base + n[0])

                return link, n

            link, _ = linker(tab)
            dve.wait_ge(s_small, 7 * 16)
            link(0, dve.tensor_scalar(lam[:, 7:8], dcol[:, :], 1.0, None, ALU.add))
            dve.tensor_scalar(skip[:, :], ident, lam[:, 7:8], None, ALU.mult).then_inc(set_dve, 1)
            dve.wait_ge(set_pe, 1)
            link(0, dve.tensor_copy(lam[:, 2:3], ps_b1[:, 0:1]))
            link(0, dve.tensor_tensor(lam[:, 3:4], lam[:, 2:3], lam[:, 2:3], ALU.mult))
            link(0, dve.tensor_scalar(lam[:, 4:5], lam[:, 3:4], 1.0, None, ALU.add))
            link(0, dve.reciprocal(lam[:, 5:6], lam[:, 4:5]))
            link(0, dve.tensor_scalar(lam[:, 6:7], lam[:, 3:4], -1.0, 1.0, ALU.mult, ALU.add))
            link(0, dve.tensor_tensor(lam[:, 0:1], lam[:, 6:7], lam[:, 5:6], ALU.mult))
            link(0, dve.tensor_scalar(lam[:, 6:7], lam[:, 2:3], -2.0, None, ALU.mult))
            link(0, dve.tensor_tensor(lam[:, 1:2], lam[:, 6:7], lam[:, 5:6], ALU.mult))
            dve.memset(cosT[:, 0:1], 1.0)
            link(0, dve.memset(sinT[:, 0:1], 0.0))
            n = 1
            while n < SEQ:
                c, s = lam[:, 0:1], lam[:, 1:2]
                dve.tensor_scalar(tmpT[:, 0, 0:n], sinT[:, 0:n], s, None, ALU.mult)
                link(0, dve.tensor_scalar(tmpT[:, 1, 0:n], cosT[:, 0:n], s, None, ALU.mult))
                dve.scalar_tensor_tensor(out=cosT[:, n:2 * n], in0=cosT[:, 0:n], scalar=c, in1=tmpT[:, 0, 0:n],
                                         op0=ALU.mult, op1=ALU.subtract)
                link(0, dve.scalar_tensor_tensor(out=sinT[:, n:2 * n], in0=sinT[:, 0:n], scalar=c,
                                                 in1=tmpT[:, 1, 0:n], op0=ALU.mult, op1=ALU.add))
                dve.tensor_tensor(lam[:, 2:3], s, s, ALU.mult)
                link(0, dve.tensor_tensor(lam[:, 3:4], c, s, ALU.mult))
                link(0, dve.scalar_tensor_tensor(out=lam[:, 0:1], in0=c, scalar=c, in1=lam[:, 2:3],
                                                 op0=ALU.mult, op1=ALU.subtract))
                link(0, dve.tensor_scalar(lam[:, 1:2], lam[:, 3:4], 2.0, None, ALU.mult))
                n *= 2

            cos2 = cosT[:, :].unsqueeze(1).to_broadcast([P, SPG, SEQ])
            sin2 = sinT[:, :].unsqueeze(1).to_broadcast([P, SPG, SEQ])
            per_e = [P, TPG, E]
            NEWTON, ROUTE = 4, 15
            T = dve.tensor_tensor

            def seqs(a):
                return a.rearrange("p (s t) -> p s t", s=SPG)

            def moments(g, st, m, mean, veps):
                me, mo, qe, qo = st[:, :, 1], st[:, :, 4], st[:, :, 2], st[:, :, 5]
                T(m[:, 0, :], me, mo, ALU.add)
                T(m[:, 1, :], me, mo, ALU.subtract)
                T(m[:, 2, :], qe, qo, ALU.add).then_inc(aggr, 1)
                dve.wait_ge(aggr, 2 * g + 1)
                dve.tensor_scalar(mean[:, :], m[:, 0, :], 0.5, None, ALU.mult)
                dve.tensor_scalar(m[:, 2, :], m[:, 2, :], 1.0 / P, EPS, ALU.mult, ALU.add)
                dve.scalar_tensor_tensor(out=m[:, 1, :], in0=m[:, 1, :], scalar=0.25, in1=m[:, 1, :],
                                         op0=ALU.mult, op1=ALU.mult).then_inc(aggr, 1)
                dve.wait_ge(aggr, 2 * g + 2)
                return T(veps[:, :], m[:, 1, :], m[:, 2, :], ALU.add)

            def refine(link, base, v, y0, t, y):
                link(base, T(t[0], y0, y0, ALU.mult))
                link(base, T(t[1], v, t[0], ALU.mult))
                link(base, dve.tensor_scalar(t[2], t[1], -0.5, 1.5, ALU.mult, ALU.add))
                link(base, T(y, t[2], y0, ALU.mult))

            def step(i, v):
                g = group(i, 1)
                if g is not None:
                    w = 1 - v
                    dve.wait_ge(r_ps, g + 1)
                    for t in range(TPG):
                        last = dve.bn_stats(st[:, t, :], ps_r[w][:, t * P:(t + 1) * P])
                    last.then_inc(stats, 1)
                    dve.wait_ge(stats, g + 1)
                    moments(g, st, mt, mean, veps).then_inc(veps_sb, 1)
                g = group(i, 3)
                if g is not None:
                    dve.wait_ge(lg_ps, g + 1)
                    T(lg[:, :, :], ps_lg[:, 0:TPG * E].rearrange("p (t e) -> p t e", e=E),
                      rbias[:, :].unsqueeze(1).to_broadcast(per_e), ALU.add).then_inc(lg_sb, 1)
                    dve.wait_ge(lg_sb, g + 1)
                    dve.reduce_max(rc[:, 0, :], lg[:, :, :], AX).then_inc(lmax, 1)
                    dve.wait_ge(lmax, g + 1)
                    T(lgs[:, :, :], lg[:, :, :], rc[:, 0, :].unsqueeze(2).to_broadcast(per_e),
                      ALU.subtract).then_inc(lgs_sb, 1)
                g = group(i, 0)
                if g is not None:
                    dve.wait_ge(b_ps, g + 1)
                    T(seqs(z1[:, :]), seqs(ps_b1[:, :]), cos2, ALU.mult)
                    T(seqs(z2[:, :]), seqs(ps_b2[:, :]), sin2, ALU.mult).then_inc(z_sb, 1)
                    dve.wait_ge(z_sb, g + 1)
                    for q in range(SPG):
                        c = slice(q * SEQ, (q + 1) * SEQ)
                        last = dve.tensor_tensor_scan(run[:, c], z1[:, c], z2[:, c], 0.0, op0=ALU.add, op1=ALU.add)
                    last.then_inc(run_sb, 1)
                    dve.wait_ge(run_sb, g + 1)
                    reused(dve, r_ps, g, 2)
                    T(seqs(hc[v]), seqs(run[:, :]), cos2, ALU.mult)
                    T(seqs(hs[v]), seqs(run[:, :]), sin2, ALU.mult).then_inc(rot_sb, 1)
                g = group(i, 2)
                if g is not None:
                    dve.wait_ge(x1T_ps, g + 1)
                    dve.wait_ge(hi_sb, g + 1)
                    reused(dve, lg_ps, g, 2)
                    free_slot(dve, lo_kept[v], g, v)
                    T(xr_lo[v][:, :], ps_x1T[:, :], xr_hi[v][:, :].bitcast(F32), ALU.subtract).then_inc(lo_sb, 1)
                g = group(i, 1)
                if g is not None:
                    w = 1 - v
                    dve.wait_ge(rs0_sb, g + 1)
                    link, n = linker(newton)
                    refine(link, g * NEWTON, veps[:, :], rs0[:, :], [nt[:, k, :] for k in range(3)], rstd[:, :])
                    assert n[0] == NEWTON
                    reused(dve, x1T_ps, g, 2)
                    free_slot(dve, x1_kept[w], g, w)
                    for t in range(TPG):
                        last = dve.tensor_scalar(x1b[w][:, t, :], ps_r[w][:, t * P:(t + 1) * P], mean[:, t:t + 1],
                                                 rstd[:, t:t + 1], ALU.subtract, ALU.mult)
                    last.then_inc(x1_sb, 1)
                g = group(i, 3)
                if g is not None:
                    dve.wait_ge(ex_sb, g + 1)
                    link, n = linker(rchain)
                    base = g * ROUTE

                    def over_e(a):
                        return a.unsqueeze(2).to_broadcast(per_e)

                    keys = first_key.unsqueeze(1).to_broadcast(per_e)
                    link(base, dve.reduce_sum(rc[:, 1, :], ex[:, :, :], AX))
                    link(base, dve.reciprocal(rc[:, 2, :], rc[:, 1, :]))
                    link(base, T(pr[:, :, :], ex[:, :, :], over_e(rc[:, 2, :]), ALU.mult))

                    def largest(p, top, best, mask):
                        link(base, dve.reduce_max(top, p, AX))
                        link(base, T(rt[:, 2, :, :], p, over_e(top), ALU.is_equal))
                        link(base, T(rt[:, 3, :, :], rt[:, 2, :, :], keys, ALU.mult))
                        link(base, dve.reduce_max(best, rt[:, 3, :, :], AX))
                        link(base, T(mask, rt[:, 3, :, :], over_e(best), ALU.is_equal))

                    largest(pr[:, :, :], rc[:, 3, :], rc[:, 4, :], rt[:, 0, :, :])
                    link(base, dve.scalar_tensor_tensor(out=pr2[:, :, :], in0=rt[:, 0, :, :], scalar=-2.0, in1=pr[:, :, :],
                                                        op0=ALU.mult, op1=ALU.add))
                    largest(pr2[:, :, :], rc[:, 5, :], rc[:, 6, :], rt[:, 1, :, :])
                    link(base, T(rt[:, 2, :, :], rt[:, 0, :, :], rt[:, 1, :, :], ALU.add))
                    assert n[0] == ROUTE
                    T(wt[:, bass.ds(g * TPG, TPG), :], pr[:, :, :], rt[:, 2, :, :], ALU.mult).then_inc(wt_sb, 1)

            pipeline(dve, step)

            for v in range(2):
                dve.wait_ge(x1_kept[v], NG * 8)
            dve.wait_ge(wt_sb, NG)

            def add(g, n, k, e):
                dve.wait_ge(y_ps, n + 1)
                if not isinstance(n, int) or n >= 1:
                    dve.wait_ge(acc_sb, n)
                if e == E:
                    x = X1[:, bass.ds(g * TPG, TPG), :].rearrange("p t d -> p (t d)")
                    T(x, ps_y[k][:, :], x, ALU.add).then_inc(acc_sb, 1)
                    return
                for t in range(TPG):
                    x = tile(X1, g * TPG + t)
                    last = dve.scalar_tensor_tensor(out=x, in0=ps_y[k][:, t * P:(t + 1) * P],
                                                    scalar=wt[:, bass.ds(g * TPG + t, 1), e],
                                                    in1=x, op0=ALU.mult, op1=ALU.add)
                last.then_inc(acc_sb, 1)

            ORDER = [E] + list(range(E))
            for m in range(2 * NX):
                add(m // NX, m, m % 2, ORDER[m % NX])
            with dve.Fori(2, NG - 1, 2) as g:
                for m in range(2 * NX):
                    add(g + m // NX, g * NX + m, m % 2, ORDER[m % NX])

            dve.wait_ge(acc_sb, NG * NX)
            with dve.Fori(0, NG) as g:
                for t in range(TPG):
                    last = dve.bn_stats(tile(sta2, g * TPG + t), tile(X1, g * TPG + t))
                last.then_inc(stats, 1)
            dve.wait_ge(stats, 2 * NG)
            moments(NG, sta2, nt2, mean2, veps2).then_inc(st2, 1)
            dve.wait_ge(rs0_sb, NG + 1)
            link, n = linker(newton)
            refine(link, NG * NEWTON, veps2[:, :], rs02[:, :], [nt2[:, k, :] for k in range(3)], rstd2[:, :])
            with dve.Fori(0, NG) as g:
                for t in range(TPG):
                    x = tile(X1, g * TPG + t)
                    last = dve.tensor_scalar(x, x, mean2[:, bass.ds(g * TPG + t, 1)],
                                             rstd2[:, bass.ds(g * TPG + t, 1)], ALU.subtract, ALU.mult)
                last.then_inc(out_sb, 1)


_INS = ['L0_attn_u', 'L0_attn_a_params', 'L0_attn_B_w', 'L0_attn_C_w', 'L0_attn_D', 'L0_ffn_router_w', 'L0_ffn_router_b',
        'L0_ffn_sw1', 'L0_ffn_sb1', 'L0_ffn_sw2', 'L0_ffn_sb2', 'L0_ffn_rw1', 'L0_ffn_rb1', 'L0_ffn_rw2', 'L0_ffn_rb2']
_OUTS = [((NSEQ, SEQ, P), 'float32')]


def kernel(**inputs):
    import numpy as _np
    import concourse.bacc as _bacc
    from concourse import mybir as _mybir
    from concourse.bass_utils import run_bass_kernel_spmd as _run

    nc = _bacc.Bacc("TRN2", target_bir_lowering=False, num_devices=1)
    arrays, args = {}, []
    for name, a in [("consts", shape_constants())] + [(n, inputs[n]) for n in _INS]:
        a = _np.ascontiguousarray(a)
        arrays[f"in_{name}_dram"] = a
        args.append(nc.dram_tensor(f"in_{name}_dram", a.shape, _mybir.dt.from_np(a.dtype), kind="ExternalInput").ap())
    for i, (shape, dtype) in enumerate(_OUTS):
        dt = _mybir.dt.from_np(_np.dtype(dtype))
        args.append(nc.dram_tensor(f"out_{i}_dram", shape, dt, kind="ExternalOutput").ap())
    build(nc, *args)
    r = _run(nc, [arrays], core_ids=[0])
    got = tuple(r.results[0][f"out_{i}_dram"] for i in range(len(_OUTS)))
    return got[0]
```

```python
from contextlib import ExitStack

import numpy as np

import concourse.bass as bass
from concourse import mybir

F32 = mybir.dt.float32
F32R = mybir.dt.float32r
BF16 = mybir.dt.bfloat16
I32 = mybir.dt.int32
U32 = mybir.dt.uint32
ALU = mybir.AluOpType
ACT = mybir.ActivationFunctionType
AX = mybir.AxisListType.X

P = 128
SEQ = 256
NSEQ = 32
GT = 512
NG = NSEQ * SEQ // GT
TPG = GT // P
SPG = GT // SEQ
E = 8
K = 2
BLK = 256
NBLK = NG * GT * K // BLK + E
CAP = NG * GT + BLK
NULLS = NBLK - NG * GT * K // BLK
ROW = P + 2
NU = NG * GT // BLK
DEPTH = 4
EARLY = NU // 2
HB = 2
HID = HB * P
B2 = 2 * HID + HB * P
B1 = B2 + P
WROW = B1 + HB
PT = 2 * TPG
QG = 4
QT = QG * TPG
SMALL, BIG = 8, 8 + E + 1
W_DONE = 5
TAB = 10 + 8 * 5
MOMENTS, RSQRT, ROUTE, SLOT = 3, 11, 15, 2
EPS = 1e-5
PEEL = 8
LAST = 14


def shape_constants():
    n = np.arange(P)
    p = np.arange(P)
    k = np.where(p <= 64, p, p - 64)
    im = p > 64
    edge = (p == 0) | (p == 64)
    ang = 2 * np.pi * np.outer(n, k) / P
    cos, sin = np.cos(ang), np.sin(ang)
    sin[:, edge] = 0
    to_basis = np.where(im, -sin, cos)
    to_turned = np.where(im, -cos, -sin)
    to_turned[:, edge] = 0
    m = np.where(edge, 1.0, 2.0)
    from_basis = np.where(im, -sin, cos) * m / P
    from_turned = np.where(im, -cos, -sin) * m / P
    from_turned[:, edge] = 0
    omega = np.zeros((P, P))
    omega[:63] = -2 * np.sin(2 * np.pi * np.outer(np.arange(1, 64), k) / P)
    omega[:, edge] = 0
    key = np.tile(E - np.arange(E), (P, 1))
    row01 = np.zeros((P, 2))
    row01[0, 0] = row01[1, 1] = 1
    before = np.triu(np.ones((P, P)), 1)
    start = np.tile(np.arange(E) * CAP, (P, 1))
    blocks = np.tile(np.arange(NBLK), (P, 1))
    meta = np.zeros((P, NG * TPG, K, 2))
    meta[..., 1] = ((np.arange(NG * TPG)[None, :] * P + n[:, None]) * K)[..., None] + np.arange(K)
    parts = {"to_basis": to_basis, "to_turned": to_turned, "from_basis": from_basis, "from_turned": from_turned,
             "ident": np.eye(P), "omega": omega, "before": before, "key": key, "row01": row01, "start": start,
             "blocks": blocks, "meta": meta.reshape(P, -1)}
    where, at = {}, 0
    for name, part in parts.items():
        where[name] = (at, at + part.shape[1])
        at += part.shape[1]
    consts = np.concatenate(list(parts.values()), axis=1).astype(np.float32)
    pads = np.zeros(((E + NULLS) * BLK, ROW), np.float32)
    pads[:, P + 1] = NG * GT * K + np.arange(len(pads))
    return consts, pads, where


def build(nc, consts, pads, u, a_params, B_w, C_w, D, router_w, router_b, sw1, sb1, sw2, sb2, rw1, rb1, rw2, rb2, out):
    where = shape_constants()[2]
    NCONST = where["meta"][0]
    x_d = u.rearrange("b s d -> (b s) d").rearrange("(g t p) d -> g p t d", p=P, t=TPG)
    out_d = out.rearrange("b s d -> (b s) d").rearrange("(g t p) d -> g p t d", p=P, t=TPG)
    xs_d = nc.dram_tensor("slot_rows", (E * CAP + NULLS * BLK, ROW), F32).ap()
    ys_d = nc.dram_tensor("results", (NG * GT * K + (E + NULLS) * BLK, P), F32).ap()
    y_d = ys_d[0:NG * GT * K, :].rearrange("(g t p k) d -> g p t (k d)", p=P, t=TPG, k=K)

    with ExitStack() as ctx:
        def sb(name, shape, dt=F32):
            return ctx.enter_context(nc.sbuf_tensor(name, shape, dt))

        def sem(name):
            return ctx.enter_context(nc.semaphore(name))

        def sems(name, n=2):
            return [sem(f"{name}{i}") for i in range(n)]

        bank = [ctx.enter_context(nc.psum_tensor(f"bank{i}", [P, 512], F32)) for i in range(8)]
        ps_xT, ps_b1, ps_b2, ps_x1T, ps_lg, ps_rank = bank[0], bank[1], bank[2], bank[3], bank[4], bank[7]
        ps_r = [bank[5], bank[6]]
        ps_t, ps_h, ps_y, ps_sh, ps_sy = bank[0:2], bank[2:4], bank[4:6], bank[6], bank[7]

        cst = sb("cst", [P, NCONST])

        def const(name):
            return cst[:, where[name][0]:where[name][1]]

        ident = const("ident")
        row0, row1 = const("row01")[:, 0:1], const("row01")[:, 1:2]
        bw = sb("bw", [P, P])
        cw = sb("cw", [P, P])
        cwT = sb("cwT", [P, P])
        apar = sb("apar", [64, 1])
        dcol = sb("dcol", [P, 1])
        rw = sb("rw", [P, E])
        rw_hi = sb("rw_hi", [P, E], F32R)
        rw_lo = sb("rw_lo", [P, E], F32R)
        rbias = sb("rbias", [P, E])
        g1T = sb("g1T", [P, P])
        g2T = sb("g2T", [P, P])
        m1T = sb("m1T", [P, P])
        m2T = sb("m2T", [P, P])
        skip = sb("skip", [P, P])
        lam = sb("lam", [P, 8])
        cosT = sb("cosT", [P, SEQ])
        sinT = sb("sinT", [P, SEQ])
        tmpT = sb("tmpT", [P, 2, SEQ // 2])
        before = sb("before", [P, P], BF16)
        allones = sb("allones", [P, P], BF16)

        wall = sb("wall", [P, E + 1, WROW])
        wshared = sb("wshared", [P, WROW], F32R)
        onesf = sb("onesf", [2, P])
        ones2 = sb("ones2", [2, P], F32R)

        xg = [sb(f"xg{i}", [P, TPG, P]) for i in range(2)]
        uT = [sb(f"uT{i}", [P, GT]) for i in range(2)]
        scan = sb("scan", [P, 3 * GT])
        z1, z2, run = (scan[:, i * GT:(i + 1) * GT] for i in range(3))
        hh = [sb(f"hh{i}", [P, HB, GT]) for i in range(2)]
        hc = [hh[i][:, 0, :] for i in range(2)]
        hs = [hh[i][:, 1, :] for i in range(2)]
        x1b = [sb(f"x1b{i}", [P, TPG, P]) for i in range(2)]
        xr_hi = [sb(f"xr_hi{i}", [P, GT], F32R) for i in range(2)]
        xr_lo = [sb(f"xr_lo{i}", [P, GT], F32R) for i in range(2)]
        st = sb("st", [P, TPG, 6])
        mt = sb("mt", [P, 3, TPG])
        mean = sb("mean", [P, TPG])
        veps = sb("veps", [P, TPG])
        rsq = sb("rsq", [P, 3, TPG])
        rstd = [sb(f"rstd{i}", [P, TPG]) for i in range(2)]
        nbias = [sb(f"nbias{i}", [P, TPG]) for i in range(2)]
        lg = sb("lg", [P, PT, E])
        lgs = sb("lgs", [P, PT, E])
        ex = sb("ex", [P, PT, E])
        pr = sb("pr", [P, PT, E])
        pr2 = sb("pr2", [P, PT, E])
        hot = sb("hot", [P, K, PT, E])
        eq = sb("eq", [P, 2, PT, E])
        rc = sb("rc", [P, 8, PT])
        chosen = sb("chosen", [P, PT + 1, E], BF16)
        rank = sb("rank", [P, PT, E])
        hrank = sb("hrank", [P, K, PT, E])
        carry = sb("carry", [P, E])
        meta = sb("meta", [P, NG * TPG, K, 2])
        slots = sb("slots", [P, NG * TPG, K])
        pay = [sb(f"pay{i}", [P, TPG, K, ROW]) for i in range(2)]
        sidx = [sb(f"sidx{i}", [P, TPG, K], U32) for i in range(2)]

        X1 = sb("X1", [P, NG * TPG, P])
        b2f = X1[0:2, NG * TPG - 10:NG * TPG - 1, :]
        b2h = X1[0:2, NG * TPG - 20:NG * TPG - 11, :]
        b1r = X1[0:(E + 1) * HB, NG * TPG - 1, :]
        x1_hi = sb("x1_hi", [P, NG * GT], F32R)
        x1_lo = sb("x1_lo", [P, NG * GT], F32R)

        bt = sb("bt", [1, 6, E])
        bti = sb("bti", [1, E], I32)
        bcmp = scan[0:1, 0:2 * NBLK * E].rearrange("p (k n e) -> p k n e", k=2, e=E)
        bsum = sb("bsum", [1, 4, NBLK])
        btab = sb("btab", [1, 2, NBLK], I32)
        pad_at = sb("pad_at", [1, E], I32)

        xs = [scan[:, i * 2 * ROW:(i + 1) * 2 * ROW].rearrange("p (j c) -> p j c", j=2) for i in range(DEPTH)]
        wb = [sb(f"wb{i}", [P, WROW], F32R)[:, :] for i in range(DEPTH)]
        xt_hi = [xr_hi[i][:, 0:BLK] for i in range(2)]
        xt_lo = [xr_lo[i][:, 0:BLK] for i in range(2)]
        hid = [hh[i][:, 0, :].rearrange("p (b n) -> p b n", b=HB) for i in range(2)]
        hid_s = hh[0][:, 1, :].rearrange("p (b n) -> p b n", b=HB)
        yo = [xg[i // 2][:, i % 2 * 2:i % 2 * 2 + 2, :] for i in range(DEPTH)]
        yidx = [sb(f"yidx{i}", [P, 2], U32) for i in range(DEPTH)]
        wrow = pay[0][:, :, :, :].rearrange("p t k c -> p (t k c)")[:, 0:NBLK * 4].rearrange("p (n j c) -> p n j c", j=2, c=2)

        yb = [(x1_hi, x1_lo)[g // (NG // 2)][:, bass.ts(g % (NG // 2), TPG * K * P)].bitcast(F32)
              .rearrange("p (t k d) -> p t k d", k=K, d=P) for g in range(NG)]
        total = [X1[:, g * TPG:(g + 1) * TPG, :] for g in range(NG)]
        st2 = cosT[:, 0:QT * 6].rearrange("p (t c) -> p t c", c=6)
        mt2 = sinT[:, 0:3 * QT].rearrange("p (c t) -> p c t", c=3)
        rsq2 = sinT[:, 3 * QT:6 * QT].rearrange("p (c t) -> p c t", c=3)
        mean2, veps2 = sinT[:, 6 * QT:7 * QT], sinT[:, 7 * QT:8 * QT]
        rstd2 = [sb(f"rstd2_{i}", [P, QT]) for i in range(2)]
        nbias2 = [sb(f"nbias2_{i}", [P, QT]) for i in range(2)]

        small_in, w_in, null_in = sem("small_in"), sem("w_in"), sem("null_in")
        x_in, x1_kept, hi_kept, lo_kept = sems("x_in"), sems("x1_kept"), sems("hi_kept"), sems("lo_kept")
        scattered = sems("scattered")
        set_pe, set_act, set_dve, w_parts, b2_step, tab = (
            sem(n) for n in ("set_pe", "set_act", "set_dve", "w_parts", "b2_step", "tab"))
        xT_ps, uT_sb, b_ps, z_sb, run_sb, rot_sb, r_ps = (
            sem(n) for n in ("xT_ps", "uT_sb", "b_ps", "z_sb", "run_sb", "rot_sb", "r_ps"))
        stats, moment, rsqrt, rstd_sb, x1_sb, x1T_ps, hi_sb, lo_sb = (
            sem(n) for n in ("stats", "moment", "rsqrt", "rstd_sb", "x1_sb", "x1T_ps", "hi_sb", "lo_sb"))
        lg_ps, lg_sb, lmax, lgs_sb, ex_sb, route, rank_ps, rank_sb, slot_step, slot_sb, pay_sb = (
            sem(n) for n in ("lg_ps", "lg_sb", "lmax", "lgs_sb", "ex_sb", "route", "rank_ps", "rank_sb",
                             "slot_step", "slot_sb", "pay_sb"))
        table, pads_in, shared_in = sem("table"), sem("pads_in"), sem("shared_in")
        xs_in, wb_in = sems("xs_in", DEPTH), sems("wb_in", DEPTH)
        xsT_ps, xt_hi_sb, xt_lo_sb, h_ps, h_sb, y_ps, y_sb, wrow_sb = (
            sem(n) for n in ("xsT_ps", "xt_hi_sb", "xt_lo_sb", "h_ps", "h_sb", "y_ps", "y_sb", "wrow_sb"))
        y_out = sems("y_out", DEPTH)
        sh_ps, sh_sb, sy_ps, sum_sb = (sem(n) for n in ("sh_ps", "sh_sb", "sy_ps", "sum_sb"))
        yb_in = sems("yb_in", NG)
        ysum_sb, total_sb, stats2, moment2, rsqrt2, norm2, out_sb, out_done = (
            sem(n) for n in ("ysum_sb", "total_sb", "stats2", "moment2", "rsqrt2", "norm2", "out_sb", "out_done"))

        keep_go, fetch_go, scatter_go, put_go = (sem(n) for n in ("keep_go", "fetch_go", "scatter_go", "put_go"))

        block = ctx.enter_context(nc.Block())

        def pipeline(eng, step):
            for i in range(-1, PEEL):
                step(i, i % 2)
            with eng.Fori(PEEL, LAST - 1, 2) as i:
                step(i, 0)
                step(i + 1, 1)
            for i in range(LAST, NG + 6):
                step(i, i % 2)

        def is_first(g, n=1):
            return isinstance(g, int) and g < n

        def group(i, lag):
            g = i - lag
            return g if not isinstance(g, int) or 0 <= g < NG else None

        def reused(eng, s, g, depth, each=1):
            if not is_first(g, depth):
                eng.wait_ge(s, (g - (depth - 1)) * each)

        def slot_count(g, v, depth=2):
            return (g - v) * (16 // depth) + 16

        def free_slot(eng, s, g, v, each=1, depth=2):
            if not is_first(g, depth):
                eng.wait_ge(s, slot_count(g - depth, v, depth) * each)

        def tile(a, n):
            return a[:, bass.ds(n, 1), :].rearrange("p o d -> p (o d)")

        def w1_part(w, low, b):
            return w[:, low * HID + b * P:low * HID + (b + 1) * P]

        def w2_block(w, b):
            return w[:, 2 * HID + b * P:2 * HID + (b + 1) * P].bitcast(F32)

        def bias2(w):
            return w[0:2, B2:B2 + P]

        def bias1(w, b):
            return w[:, B1 + b:B1 + b + 1].bitcast(F32)

        def blocks(eng, step):
            for n in range(DEPTH):
                step(n, n, EARLY)
            with eng.Fori(1, NU - EARLY) as k:
                for q in range(DEPTH):
                    step(k * DEPTH + q, q, k + EARLY)
            for n in range(DEPTH * (NU - EARLY), NBLK):
                step(n, n % DEPTH, None)

        @block.sync
        def _(sp):
            small = [(cst[:, :], consts[:, 0:NCONST]), (bw[:, :], B_w), (cw[:, :], C_w),
                     (apar[:, :], a_params.rearrange("(p o) -> p o", o=1)),
                     (dcol[:, :], D.rearrange("(p o) -> p o", o=1)),
                     (rw[:, :], router_w), (rbias[:, :], router_b.partition_broadcast(P)),
                     (meta[:, :, :, :].rearrange("p t k c -> p (t k c)"), consts[:, NCONST:])]
            assert len(small) == SMALL
            for dst, src in small:
                sp.dma_start(dst, src).then_inc(small_in, 16)
            for g in range(2):
                sp.dma_start(xg[g][:, :, :], x_d[g]).then_inc(x_in[g], 16)
            big = [(wall[:, 0:E, HID:2 * HID], rw1.rearrange("e d h -> d e h")), (wall[:, E, HID:2 * HID], sw1),
                   (b1r[0:E * HB, :], rb1.rearrange("e (b h) -> (e b) h", b=HB)),
                   (b1r[E * HB:, :], sb1.rearrange("(b h) -> b h", b=HB)),
                   (b2f[0:1, 0:E, :], rb2.unsqueeze(0)), (b2f[1:2, 0:E, :], rb2.unsqueeze(0)),
                   (b2f[0:1, E, :], sb2.unsqueeze(0)), (b2f[1:2, E, :], sb2.unsqueeze(0))]
            for e in range(E + 1):
                src = sw2 if e == E else rw2[e]
                big.append((wall[:, e, 2 * HID:2 * HID + HB * P].rearrange("p (b d) -> p b d", b=HB),
                            src.rearrange("(b h) d -> h b d", b=HB)))
            assert len(big) == BIG
            for dst, src in big:
                sp.dma_start(dst, src).then_inc(w_in, 16)
            sp.dma_start(xs_d[E * CAP:, :], pads[E * BLK:, :]).then_inc(null_in, 16)

            def step(i, v):
                g = group(i, -2)
                if g is not None and not is_first(g, 2):
                    sp.wait_ge(xT_ps, g - 1)
                    sp.dma_start(xg[v][:, :, :], x_d[bass.ds(g, 1)].rearrange("o p t d -> (o p) t d")).then_inc(x_in[v], 16)
                g = group(i, 2)
                if g is not None:
                    sp.wait_ge(x1_sb, g + 1)
                    if isinstance(g, int) and g == PEEL - 3:
                        sp.wait_ge(w_parts, W_DONE)
                        sp.wait_ge(set_pe, 4)
                    sp.dma_start(X1[:, bass.ds(g * TPG, TPG), :], x1b[v][:, :, :]).then_inc(x1_kept[v], 16)
                g = group(i, 3)
                if g is not None:
                    w = 1 - v
                    sp.wait_ge(hi_sb, g + 1)
                    sp.dma_start(x1_hi[:, bass.ds(g * GT, GT)].bitcast(F32), xr_hi[w][:, :].bitcast(F32)).then_inc(hi_kept[w], 16)
                    sp.wait_ge(lo_sb, g + 1)
                    sp.sem_inc(keep_go, 1)
                    sp.dma_start(x1_lo[:, bass.ds(g * GT, GT)].bitcast(F32), xr_lo[w][:, :].bitcast(F32)).then_inc(lo_kept[w], 16)

            pipeline(sp, step)

            sp.wait_ge(w_parts, W_DONE)
            sp.dma_start(wshared[:, :].bitcast(F32), wall[:, E, :]).then_inc(shared_in, 16)
            sp.wait_ge(table, 1)
            for e in range(E):
                at = sp.value_load(pad_at[0:1, e:e + 1], min_val=e * CAP, max_val=(e + 1) * CAP - BLK)
                sp.dma_start(xs_d[bass.ds(at, BLK), :], pads[e * BLK:(e + 1) * BLK, :]).then_inc(pads_in, 16)
            for v in range(2):
                sp.wait_ge(scattered[v], TPG * K * NG * 8)
            sp.wait_ge(pads_in, E * 16)
            sp.wait_ge(null_in, 16)
            sp.wait_ge(table, 2)
            def fetch(n, q, s):
                row = sp.value_load(btab[0:1, 0, bass.ds(n, 1)], min_val=0, max_val=E * CAP + (NULLS - 1) * BLK)
                e = sp.value_load(btab[0:1, 1, bass.ds(n, 1)], min_val=0, max_val=E - 1)
                reused(sp, xsT_ps, n, DEPTH)
                reused(sp, wrow_sb, n, DEPTH)
                sp.sem_inc(fetch_go, 1)
                sp.dma_start(xs[q], xs_d[bass.ds(row, BLK), :].rearrange("(j p) c -> p j c", p=P)).then_inc(xs_in[q], 16)
                reused(sp, h_sb, n, DEPTH)
                reused(sp, y_ps, n, DEPTH)
                sp.sem_inc(fetch_go, 1)
                sp.dma_start(wb[q].bitcast(F32), wall[:, bass.ds(e, 1), :].rearrange("p o c -> p (o c)")).then_inc(wb_in[q], 16)

            blocks(sp, fetch)

            for q in range(DEPTH):
                sp.wait_ge(y_out[q], 2 * NBLK * 16 // DEPTH)

            for g in range(NG):
                sp.dma_start(yb[g].rearrange("p t k d -> p t (k d)"), y_d[g]).then_inc(yb_in[g], 16)
            sp.wait_ge(out_done, NG * 16)

        @block.tensor
        def _(pe):
            mm = pe.matmul
            pe.wait_ge(small_in, SMALL * 16)
            mm(ps_b1[:, 0:1], const("omega")[0:63, :], apar[0:63, :], start=True, stop=True).then_inc(set_pe, 1)
            mm(ps_b2[:, 0:P], bw[:, :], const("to_basis"), start=True, stop=True)
            mm(ps_b2[:, P:2 * P], bw[:, :], const("to_turned"), start=True, stop=True)
            pe.transpose(ps_b2[:, 2 * P:3 * P], cw[:, :], ident).then_inc(set_pe, 1)
            pe.wait_ge(set_act, 1)
            mm(ps_x1T[:, 0:P], const("from_basis"), cwT[:, :], start=True, stop=True)
            mm(ps_x1T[:, P:2 * P], const("from_turned"), cwT[:, :], start=True, stop=True).then_inc(set_pe, 1)
            pe.wait_ge(w_in, BIG * 16)
            pe.transpose(ps_lg[:, 0:(E + 1) * HB], b1r[:, :], ident[0:(E + 1) * HB, 0:(E + 1) * HB]).then_inc(set_pe, 1)

            def step(i, v):
                w = 1 - v
                g = group(i, 0)
                if g is not None:
                    pe.wait_ge(uT_sb, g + 1)
                    if is_first(g):
                        pe.wait_ge(set_act, 2)
                        pe.wait_ge(tab, 2)
                    reused(pe, z_sb, g, 1)
                    mm(ps_b1[:, :], g1T[:, :], uT[v][:, :], start=True, stop=True)
                    mm(ps_b2[:, :], g2T[:, :], uT[v][:, :], start=True, stop=True).then_inc(b_ps, 1)
                g = group(i, 1)
                if g is not None:
                    pe.wait_ge(rot_sb, g + 1)
                    if is_first(g):
                        pe.wait_ge(set_act, 3)
                        pe.wait_ge(set_dve, 1)
                    reused(pe, x1_sb, g, 2)
                    for t in range(TPG):
                        c = slice(t * P, (t + 1) * P)
                        mm(ps_r[w][:, c], hc[w][:, c], m1T[:, :], start=True, stop=False)
                        mm(ps_r[w][:, c], hs[w][:, c], m2T[:, :], start=False, stop=False)
                        last = mm(ps_r[w][:, c], uT[w][:, c], skip[:, :], start=False, stop=True)
                    last.then_inc(r_ps, 1)
                g = group(i, 3)
                if g is not None:
                    pe.wait_ge(hi_sb, g + 1)
                    pe.wait_ge(lo_sb, g + 1)
                    if is_first(g):
                        pe.wait_ge(set_act, 4)
                        pe.wait_ge(w_parts, 2)
                    if w == 0 and not is_first(g, 2):
                        pe.wait_ge(lg_sb, g)
                    for t in range(TPG):
                        c = slice(t * P, (t + 1) * P)
                        o = ps_lg[:, (w * TPG + t) * E:(w * TPG + t + 1) * E]
                        mm(o, xr_hi[w][:, c], rw_hi[:, :], start=True, stop=False)
                        mm(o, xr_hi[w][:, c], rw_lo[:, :], start=False, stop=False)
                        last = mm(o, xr_lo[w][:, c], rw_hi[:, :], start=False, stop=True)
                    last.then_inc(lg_ps, 1)
                g = group(i, 2)
                if g is not None:
                    pe.wait_ge(x1_sb, g + 1)
                    if is_first(g):
                        pe.wait_ge(set_act, 3)
                    reused(pe, lo_sb, g, 1)
                    reused(pe, hi_sb, g, 1)
                    for t in range(TPG):
                        last = pe.transpose(ps_x1T[:, t * P:(t + 1) * P], x1b[v][:, t, :], ident)
                    last.then_inc(x1T_ps, 1)
                g = group(i, -1)
                if g is not None:
                    pe.wait_ge(x_in[w], slot_count(g, w))
                    reused(pe, uT_sb, g, 1)
                    for t in range(TPG):
                        last = pe.transpose(ps_xT[:, t * P:(t + 1) * P], xg[w][:, t, :], ident)
                    last.then_inc(xT_ps, 1)
                g = group(i, 5) if v else None
                if g is not None:
                    pe.wait_ge(route, (g + 2) * ROUTE)
                    reused(pe, rank_sb, g, 1)
                    mm(ps_rank[:, 0:(PT + 1) * E], before[:, :], chosen[:, :, :].rearrange("p t e -> p (t e)"), start=True, stop=False)
                    for t in range(PT):
                        last = mm(ps_rank[:, (t + 1) * E:(PT + 1) * E].rearrange("p (t e) -> p t e", e=E), allones[:, :],
                                  chosen[:, t, :].unsqueeze(1).to_broadcast([P, PT - t, E]), start=False, stop=t == PT - 1)
                    last.then_inc(rank_ps, 2)

            pipeline(pe, step)

            for s in (uT_sb, z_sb, x1_sb, hi_sb, lo_sb, lg_sb, rank_sb):
                pe.wait_ge(s, NG)
            for v in range(2):
                pe.wait_ge(hi_kept[v], NG * 8)
                pe.wait_ge(lo_kept[v], NG * 8)
            pe.wait_ge(shared_in, 16)

            def split3(o, w, b, xh, xl):
                mm(o, w1_part(w, 0, b), xh, start=True, stop=False)
                mm(o, w1_part(w, 1, b), xh, start=False, stop=False)
                return mm(o, w1_part(w, 0, b), xl, start=False, stop=True)

            def second(ps, h, w):
                for j in range(BLK // P):
                    o = ps[:, j * P:(j + 1) * P]
                    mm(o, ones2[:, :], bias2(w), start=True, stop=False)
                    for b in range(HB):
                        last = mm(o, h[:, b, j * P:(j + 1) * P], w2_block(w, b), start=False, stop=b == HB - 1)
                return last

            def turn(n, q):
                pe.wait_ge(xs_in[q], slot_count(n, q, DEPTH))
                reused(pe, xt_hi_sb, n, 2)
                reused(pe, xt_lo_sb, n, 2)
                for j in range(2):
                    last = pe.transpose(ps_t[q % 2][:, j * P:(j + 1) * P], xs[q][:, j, 0:P], ident)
                last.then_inc(xsT_ps, 1)

            def first_layer(n, q):
                v = q % 2
                pe.wait_ge(wb_in[q], slot_count(n, q, DEPTH))
                pe.wait_ge(xt_hi_sb, n + 1)
                pe.wait_ge(xt_lo_sb, n + 1)
                reused(pe, h_sb, n, 2)
                for b in range(HB):
                    last = split3(ps_h[v][:, b * BLK:(b + 1) * BLK], wb[q], b, xt_hi[v], xt_lo[v])
                last.then_inc(h_ps, 1)

            def second_layer(n, q):
                pe.wait_ge(h_sb, n + 1)
                reused(pe, y_sb, n, 2)
                second(ps_y[q % 2], hid[q % 2], wb[q]).then_inc(y_ps, 1)

            def shared_first(s):
                reused(pe, sh_sb, s, 1)
                c = bass.ds(s * BLK, BLK)
                for b in range(HB):
                    last = split3(ps_sh[:, b * BLK:(b + 1) * BLK], wshared[:, :], b, x1_hi[:, c], x1_lo[:, c])
                last.then_inc(sh_ps, 1)

            def shared_second(s):
                pe.wait_ge(sh_sb, s + 1)
                reused(pe, sum_sb, s, 1)
                second(ps_sy, hid_s, wshared[:, :]).then_inc(sy_ps, 1)

            def step(n, q, s):
                if not isinstance(n, int) or n + 1 < NBLK:
                    turn(n + 1, (q + 1) % DEPTH)
                first_layer(n, q)
                if not is_first(n):
                    second_layer(n - 1, (q - 1) % DEPTH)
                if s is not None and q == 0:
                    shared_first(s)
                if s is not None and q == 2:
                    shared_second(s)

            shared_first(0)
            with pe.Fori(1, EARLY) as s:
                shared_first(s)
                shared_second(s - 1)
            shared_second(EARLY - 1)
            turn(0, 0)
            blocks(pe, step)
            second_layer(NBLK - 1, (NBLK - 1) % DEPTH)

        @block.gpsimd
        def _(pool):
            pool.wait_ge(small_in, SMALL * 16)
            pool.tensor_copy(rw_hi[:, :], rw[:, :]).then_inc(w_parts, 1)
            pool.wait_ge(w_parts, 1)
            pool.tensor_tensor(rw_lo[:, :], rw[:, :], rw_hi[:, :].bitcast(F32), ALU.subtract).then_inc(w_parts, 1)
            pool.memset(onesf[:, :], 1.0).then_inc(w_parts, 1)
            pool.memset(wall[:, :, B2:B2 + P], 0.0).then_inc(w_parts, 1)
            pool.wait_ge(w_in, BIG * 16)
            pool.wait_ge(w_parts, 4)
            pool.tensor_copy(ones2[:, :], onesf[:, :])
            pool.tensor_copy(wall[:, :, 0:HID].bitcast(F32R), wall[:, :, HID:2 * HID])
            pool.tensor_copy(b2h[:, :, :].bitcast(F32R), b2f[:, :, :]).then_inc(b2_step, 1)
            pool.wait_ge(b2_step, 1)
            lo = wall[:, :, HID:2 * HID]
            pool.tensor_tensor(lo.bitcast(F32R), lo, wall[:, :, 0:HID], ALU.subtract)
            pool.tensor_tensor(b2f[:, :, :], b2f[:, :, :], b2h[:, :, :], ALU.subtract).then_inc(b2_step, 1)
            pool.wait_ge(b2_step, 2)
            pool.tensor_scalar(b2f[:, :, :], b2f[:, :, :], row1[0:2, :], None, ALU.mult)
            pool.tensor_scalar(b2h[:, :, :], b2h[:, :, :], row0[0:2, :], None, ALU.mult).then_inc(b2_step, 1)
            pool.wait_ge(b2_step, 3)
            pool.wait_ge(w_parts, 4)
            pool.tensor_tensor(wall[0:2, :, B2:B2 + P].bitcast(F32R), b2h[:, :, :], b2f[:, :, :], ALU.add).then_inc(w_parts, 1)

            def scatter(g, v):
                pool.wait_ge(pay_sb, g + 1)
                pool.sem_inc(scatter_go, 1)
                for t in range(TPG):
                    for k in range(K):
                        pool.indirect_dma_start(xs_d, bass.IndirectOffsetOnAxis(ap=sidx[v][:, t, k:k + 1], axis=0),
                                                pay[v][:, t, k, :], None).then_inc(scattered[v], 16)

            with pool.Fori(0, NG - 1, 2) as g:
                scatter(g, 0)
                scatter(g + 1, 1)

            def put(n, q):
                pool.wait_ge(y_sb, n + 1)
                pool.sem_inc(put_go, 1)
                for j in range(2):
                    pool.indirect_dma_start(ys_d, bass.IndirectOffsetOnAxis(ap=yidx[q][:, j:j + 1], axis=0),
                                            yo[q][:, j, :], None).then_inc(y_out[q], 16)

            with pool.Fori(0, NBLK // DEPTH) as k:
                for q in range(DEPTH):
                    put(k * DEPTH + q, q)

            pool.wait_ge(sum_sb, NU)
            for g in range(NG):
                pool.wait_ge(yb_in[g], 16)
                pool.tensor_tensor(total[g], total[g], yb[g][:, :, 0, :], ALU.add).then_inc(ysum_sb, 1)

        @block.scalar
        def _(act):
            act.wait_ge(set_pe, 2)
            act.copy(cwT[:, :], ps_b2[:, 2 * P:3 * P]).then_inc(set_act, 1)
            act.copy(g1T[:, :], ps_b2[:, 0:P])
            act.copy(g2T[:, :], ps_b2[:, P:2 * P]).then_inc(set_act, 1)
            act.wait_ge(set_pe, 3)
            act.copy(m1T[:, :], ps_x1T[:, 0:P])
            act.copy(m2T[:, :], ps_x1T[:, P:2 * P]).then_inc(set_act, 1)
            act.wait_ge(set_pe, 4)
            act.copy(wall[:, :, B1:B1 + HB], ps_lg[:, 0:(E + 1) * HB].rearrange("p (e b) -> p e b", b=HB)).then_inc(set_act, 1)

            def step(i, v):
                w = 1 - v
                g = group(i, 2)
                if g is not None:
                    act.wait_ge(x1T_ps, g + 1)
                    reused(act, lg_ps, g, 2)
                    free_slot(act, hi_kept[v], g, v)
                    act.copy(xr_hi[v][:, :], ps_x1T[:, :]).then_inc(hi_sb, 1)
                g = group(i, -1)
                if g is not None:
                    act.wait_ge(xT_ps, g + 1)
                    reused(act, r_ps, g, 2)
                    act.copy(uT[w][:, :], ps_xT[:, :]).then_inc(uT_sb, 1)
                g = group(i, 6)
                if g is not None:
                    act.wait_ge(slot_sb, g + (2 - v))
                    act.wait_ge(x1_kept[v], slot_count(g, v))
                    free_slot(act, scattered[v], g, v, TPG * K)
                    c = bass.ds(g * TPG, TPG)
                    act.copy(pay[v][:, :, :, 0:P], X1[:, c, :].unsqueeze(2).to_broadcast([P, TPG, K, P]))
                    act.copy(pay[v][:, :, :, P:ROW], meta[:, c, :, :])
                    act.copy(sidx[v][:, :, :], slots[:, c, :]).then_inc(pay_sb, 1)
                g = group(i, 4) if v == 0 else None
                if g is not None:
                    act.wait_ge(lgs_sb, g + 2)
                    if not is_first(g, 2):
                        act.wait_ge(route, g * ROUTE)
                    act.activation(ex[:, :, :], lgs[:, :, :], ACT.Exp).then_inc(ex_sb, 2)
                g = group(i, 1)
                if g is not None:
                    act.wait_ge(rstd_sb, g + 1)
                    reused(act, x1T_ps, g, 2)
                    free_slot(act, x1_kept[w], g, w)
                    for t in range(TPG):
                        last = act.activation(x1b[w][:, t, :], ps_r[w][:, t * P:(t + 1) * P], ACT.Identity,
                                              bias=nbias[w][:, t:t + 1], scale=rstd[w][:, t:t + 1])
                    last.then_inc(x1_sb, 1)

            pipeline(act, step)
            act.wait_ge(r_ps, NG)
            act.wait_ge(lg_ps, NG)
            for v in range(2):
                act.wait_ge(hi_kept[v], NG * 8)

            def step(n, q, s):
                if not isinstance(n, int) or n + 1 < NBLK:
                    high(n + 1, (q + 1) % 2)
                hidden(n, q)
                if s is not None and q == 0:
                    shared_hidden(s)

            def shared_hidden(s):
                act.wait_ge(sh_ps, s + 1)
                reused(act, sy_ps, s, 1)
                for b in range(HB):
                    last = act.activation(hid_s[:, b, :], ps_sh[:, b * BLK:(b + 1) * BLK], ACT.Gelu, bias=bias1(wshared[:, :], b))
                last.then_inc(sh_sb, 1)

            def high(n, v):
                act.wait_ge(xsT_ps, n + 1)
                reused(act, h_ps, n, 2)
                act.copy(xt_hi[v], ps_t[v][:, 0:BLK]).then_inc(xt_hi_sb, 1)

            def hidden(n, q):
                v = q % 2
                act.wait_ge(h_ps, n + 1)
                reused(act, y_ps, n, 2)
                for b in range(HB):
                    last = act.activation(hid[v][:, b, :], ps_h[v][:, b * BLK:(b + 1) * BLK], ACT.Gelu, bias=bias1(wb[q], b))
                last.then_inc(h_sb, 1)

            shared_hidden(0)
            with act.Fori(1, EARLY) as s:
                shared_hidden(s)
            high(0, 0)
            blocks(act, step)

            for g in range(NG):
                act.wait_ge(norm2, g // QG + 1)
                for t in range(TPG):
                    c = slice(g % QG * TPG + t, g % QG * TPG + t + 1)
                    x, v = total[g][:, t, :], g // QG % 2
                    last = act.activation(x, x, ACT.Identity, bias=nbias2[v][:, c], scale=rstd2[v][:, c])
                last.then_inc(out_sb, 1)
                act.wait_ge(out_sb, g + 1)
                act.dma_start(out_d[g], total[g]).then_inc(out_done, 16)

        @block.vector
        def _(dve):
            T = dve.tensor_tensor

            def linker(s, inc=1):
                n = [0]

                def link(base, ins):
                    n[0] += inc
                    ins.then_inc(s, inc)
                    dve.wait_ge(s, base + n[0])

                return link, n

            link, links = linker(tab)
            dve.wait_ge(small_in, SMALL * 16)
            link(0, dve.tensor_scalar(lam[:, 7:8], dcol[:, :], 1.0, None, ALU.add))
            dve.tensor_scalar(skip[:, :], ident, lam[:, 7:8], None, ALU.mult)
            dve.tensor_copy(before[:, :], const("before"))
            dve.memset(allones[:, :], 1.0)
            dve.memset(chosen[:, PT, :], 0.0)
            dve.tensor_copy(carry[:, :], const("start")).then_inc(set_dve, 1)
            dve.wait_ge(set_pe, 1)
            link(0, dve.tensor_copy(lam[:, 2:3], ps_b1[:, 0:1]))
            link(0, T(lam[:, 3:4], lam[:, 2:3], lam[:, 2:3], ALU.mult))
            link(0, dve.tensor_scalar(lam[:, 4:5], lam[:, 3:4], 1.0, None, ALU.add))
            link(0, dve.reciprocal(lam[:, 5:6], lam[:, 4:5]))
            link(0, dve.tensor_scalar(lam[:, 6:7], lam[:, 3:4], -1.0, 1.0, ALU.mult, ALU.add))
            link(0, T(lam[:, 0:1], lam[:, 6:7], lam[:, 5:6], ALU.mult))
            link(0, dve.tensor_scalar(lam[:, 6:7], lam[:, 2:3], -2.0, None, ALU.mult))
            link(0, T(lam[:, 1:2], lam[:, 6:7], lam[:, 5:6], ALU.mult))
            dve.memset(cosT[:, 0:1], 1.0)
            link(0, dve.memset(sinT[:, 0:1], 0.0))
            n = 1
            while n < SEQ:
                c, s = lam[:, 0:1], lam[:, 1:2]
                dve.tensor_scalar(tmpT[:, 0, 0:n], sinT[:, 0:n], s, None, ALU.mult)
                link(0, dve.tensor_scalar(tmpT[:, 1, 0:n], cosT[:, 0:n], s, None, ALU.mult))
                dve.scalar_tensor_tensor(out=cosT[:, n:2 * n], in0=cosT[:, 0:n], scalar=c, in1=tmpT[:, 0, 0:n],
                                         op0=ALU.mult, op1=ALU.subtract)
                link(0, dve.scalar_tensor_tensor(out=sinT[:, n:2 * n], in0=sinT[:, 0:n], scalar=c,
                                                 in1=tmpT[:, 1, 0:n], op0=ALU.mult, op1=ALU.add))
                T(lam[:, 2:3], s, s, ALU.mult)
                link(0, T(lam[:, 3:4], c, s, ALU.mult))
                link(0, dve.scalar_tensor_tensor(out=lam[:, 0:1], in0=c, scalar=c, in1=lam[:, 2:3],
                                                 op0=ALU.mult, op1=ALU.subtract))
                link(0, dve.tensor_scalar(lam[:, 1:2], lam[:, 3:4], 2.0, None, ALU.mult))
                n *= 2

            assert links[0] == TAB
            cos2 = cosT[:, :].unsqueeze(1).to_broadcast([P, SPG, SEQ])
            sin2 = sinT[:, :].unsqueeze(1).to_broadcast([P, SPG, SEQ])
            per_e = [P, PT, E]

            def seqs(a):
                return a.rearrange("p (s t) -> p s t", s=SPG)

            def moments(s, g, st, m, mean, veps):
                link, n = linker(s)
                base = g * MOMENTS
                me, mo, qe, qo = st[:, :, 1], st[:, :, 4], st[:, :, 2], st[:, :, 5]
                T(m[:, 0, :], me, mo, ALU.add)
                T(m[:, 1, :], me, mo, ALU.subtract)
                link(base, T(m[:, 2, :], qe, qo, ALU.add))
                dve.tensor_scalar(mean[:, :], m[:, 0, :], 0.5, None, ALU.mult)
                dve.tensor_scalar(m[:, 2, :], m[:, 2, :], 1.0 / P, EPS, ALU.mult, ALU.add)
                link(base, dve.scalar_tensor_tensor(out=m[:, 1, :], in0=m[:, 1, :], scalar=0.25, in1=m[:, 1, :],
                                                    op0=ALU.mult, op1=ALU.mult))
                link(base, T(veps[:, :], m[:, 1, :], m[:, 2, :], ALU.add))
                assert n[0] == MOMENTS

            def reciprocal_root(s, g, x, t, y):
                link, n = linker(s)
                base = g * RSQRT
                link(base, dve.tensor_scalar(t[:, 0, :].bitcast(I32), x.bitcast(I32), 1, None, ALU.logical_shift_right))
                link(base, dve.tensor_scalar(t[:, 1, :].bitcast(I32), t[:, 0, :].bitcast(I32), -1.0, float(0x5F3759DF), ALU.mult, ALU.add))
                for k in range(3):
                    link(base, T(t[:, 0, :], t[:, 1, :], t[:, 1, :], ALU.mult))
                    link(base, dve.scalar_tensor_tensor(out=t[:, 2, :], in0=t[:, 0, :], scalar=-0.5, in1=x, op0=ALU.mult, op1=ALU.mult))
                    o = y if k == 2 else t[:, 1, :]
                    link(base, dve.scalar_tensor_tensor(out=o, in0=t[:, 2, :], scalar=1.5, in1=t[:, 1, :], op0=ALU.add, op1=ALU.mult))
                assert n[0] == RSQRT

            def step(i, v):
                w = 1 - v
                g = group(i, 0)
                if g is not None:
                    dve.wait_ge(b_ps, g + 1)
                    T(seqs(z1), seqs(ps_b1[:, :]), cos2, ALU.mult)
                    T(seqs(z2), seqs(ps_b2[:, :]), sin2, ALU.mult).then_inc(z_sb, 1)
                    dve.wait_ge(z_sb, g + 1)
                    for q in range(SPG):
                        c = slice(q * SEQ, (q + 1) * SEQ)
                        last = dve.tensor_tensor_scan(run[:, c], z1[:, c], z2[:, c], 0.0, op0=ALU.add, op1=ALU.add)
                    last.then_inc(run_sb, 1)
                    dve.wait_ge(run_sb, g + 1)
                    reused(dve, r_ps, g, 2)
                    T(seqs(hc[v]), seqs(run), cos2, ALU.mult)
                    T(seqs(hs[v]), seqs(run), sin2, ALU.mult).then_inc(rot_sb, 1)
                g = group(i, 2)
                if g is not None:
                    dve.wait_ge(x1T_ps, g + 1)
                    dve.wait_ge(hi_sb, g + 1)
                    reused(dve, lg_ps, g, 2)
                    free_slot(dve, lo_kept[v], g, v)
                    T(xr_lo[v][:, :], ps_x1T[:, :], xr_hi[v][:, :].bitcast(F32), ALU.subtract).then_inc(lo_sb, 1)
                g = group(i, 4) if v == 0 else None
                if g is not None:
                    dve.wait_ge(lg_ps, g + 2)
                    T(lg[:, :, :], ps_lg[:, 0:PT * E].rearrange("p (t e) -> p t e", e=E),
                      rbias[:, :].unsqueeze(1).to_broadcast(per_e), ALU.add).then_inc(lg_sb, 2)
                    dve.wait_ge(lg_sb, g + 2)
                    dve.reduce_max(rc[:, 0, :], lg[:, :, :], AX).then_inc(lmax, 2)
                    dve.wait_ge(lmax, g + 2)
                    T(lgs[:, :, :], lg[:, :, :], rc[:, 0, :].unsqueeze(2).to_broadcast(per_e),
                      ALU.subtract).then_inc(lgs_sb, 2)
                g = group(i, 1)
                if g is not None:
                    dve.wait_ge(r_ps, g + 1)
                    for t in range(TPG):
                        last = dve.bn_stats(st[:, t, :], ps_r[w][:, t * P:(t + 1) * P])
                    last.then_inc(stats, 1)
                    dve.wait_ge(stats, g + 1)
                    moments(moment, g, st, mt, mean, veps)
                    reused(dve, x1_sb, g, 2)
                    reciprocal_root(rsqrt, g, veps[:, :], rsq, rstd[w][:, :])
                    dve.scalar_tensor_tensor(out=nbias[w][:, :], in0=mean[:, :], scalar=-1.0, in1=rstd[w][:, :],
                                             op0=ALU.mult, op1=ALU.mult).then_inc(rstd_sb, 1)
                g = group(i, 4) if v == 0 else None
                if g is not None:
                    dve.wait_ge(ex_sb, g + 2)
                    link, n = linker(route, 2)
                    base = g * ROUTE

                    def over_e(a):
                        return a.unsqueeze(2).to_broadcast(per_e)

                    keys = const("key").unsqueeze(1).to_broadcast(per_e)
                    link(base, dve.reduce_sum(rc[:, 1, :], ex[:, :, :], AX))
                    link(base, dve.reciprocal(rc[:, 2, :], rc[:, 1, :]))
                    link(base, T(pr[:, :, :], ex[:, :, :], over_e(rc[:, 2, :]), ALU.mult))

                    def largest(p, top, best, mask):
                        link(base, dve.reduce_max(top, p, AX))
                        link(base, T(eq[:, 0, :, :], p, over_e(top), ALU.is_equal))
                        link(base, T(eq[:, 1, :, :], eq[:, 0, :, :], keys, ALU.mult))
                        link(base, dve.reduce_max(best, eq[:, 1, :, :], AX))
                        link(base, T(mask, eq[:, 1, :, :], over_e(best), ALU.is_equal))

                    largest(pr[:, :, :], rc[:, 3, :], rc[:, 5, :], hot[:, 0, :, :])
                    link(base, dve.scalar_tensor_tensor(out=pr2[:, :, :], in0=hot[:, 0, :, :], scalar=-2.0, in1=pr[:, :, :],
                                                        op0=ALU.mult, op1=ALU.add))
                    largest(pr2[:, :, :], rc[:, 4, :], rc[:, 6, :], hot[:, 1, :, :])
                    if not is_first(g, 2):
                        dve.wait_ge(rank_ps, g)
                    dve.tensor_copy(meta[:, bass.ds(g * TPG, PT), :, 0].rearrange("p t k -> p k t"), rc[:, 3:5, :])
                    link(base, T(chosen[:, 0:PT, :], hot[:, 0, :, :], hot[:, 1, :, :], ALU.add))
                    assert n[0] == 2 * ROUTE
                g = group(i, 5) if v else None
                if g is not None:
                    dve.wait_ge(rank_ps, g + 2)
                    link, n = linker(slot_step, 2)
                    base = g * SLOT
                    ps = ps_rank[:, 0:(PT + 1) * E].rearrange("p (t e) -> p t e", e=E)
                    link(base, T(rank[:, :, :], ps[:, 0:PT, :], carry[:, :].unsqueeze(1).to_broadcast(per_e), ALU.add))
                    T(carry[:, :], ps[:, PT, :], carry[:, :], ALU.add).then_inc(rank_sb, 2)
                    link(base, T(hrank[:, :, :, :], hot[:, :, :, :], rank[:, :, :].unsqueeze(1).to_broadcast([P, K, PT, E]), ALU.mult))
                    assert n[0] == 2 * SLOT
                    dve.reduce_sum(slots[:, bass.ds(g * TPG, PT), :].rearrange("p t k -> p k t"), hrank[:, :, :, :], AX).then_inc(slot_sb, 2)

            pipeline(dve, step)

            link, n = linker(tab)
            base = TAB
            c, nb, upto, cnt = (bt[:, k, :] for k in range(4))
            dve.wait_ge(rank_sb, NG)
            dve.tensor_copy(pad_at[:, :], carry[0:1, :]).then_inc(table, 1)
            link(base, T(cnt, carry[0:1, :], const("start")[0:1, :], ALU.subtract))
            link(base, dve.tensor_scalar(bti[:, :], cnt, float(BLK - 1), None, ALU.add))
            link(base, dve.tensor_scalar(bti[:, :], bti[:, :], 8, None, ALU.logical_shift_right))
            link(base, dve.tensor_copy(nb, bti[:, :]))
            link(base, dve.memset(c, 0.0))
            link(base, dve.tensor_tensor_scan(upto, nb, c, 0.0, op0=ALU.add, op1=ALU.add))
            be = [1, NBLK, E]
            link(base, T(bcmp[:, 0, :, :], const("blocks")[0:1, :].unsqueeze(2).to_broadcast(be),
                         upto.unsqueeze(1).to_broadcast(be), ALU.is_ge))
            link(base, T(bcmp[:, 1, :, :], bcmp[:, 0, :, :], nb.unsqueeze(1).to_broadcast(be), ALU.mult))
            link(base, dve.reduce_sum(bsum[:, 0:2, :], bcmp[:, :, :, :], AX))
            link(base, T(bsum[:, 2, :], const("blocks")[0:1, :], bsum[:, 1, :], ALU.subtract))
            link(base, dve.tensor_scalar(bsum[:, 3, :], bsum[:, 0, :], float(CAP), None, ALU.mult))
            link(base, dve.scalar_tensor_tensor(out=btab[:, 0, :], in0=bsum[:, 2, :], scalar=float(BLK), in1=bsum[:, 3, :],
                                                op0=ALU.mult, op1=ALU.add))
            dve.tensor_scalar(btab[:, 1, :], bsum[:, 0, :], float(E - 1), None, ALU.min).then_inc(table, 1)

            for v in range(2):
                dve.wait_ge(x1_kept[v], NG * 8)
                dve.wait_ge(lo_kept[v], NG * 8)
            dve.wait_ge(lg_ps, NG)
            dve.wait_ge(xT_ps, NG)
            dve.wait_ge(pay_sb, NG)

            def step(n, q, s):
                if not isinstance(n, int) or n + 1 < NBLK:
                    low(n + 1, (q + 1) % DEPTH)
                if not is_first(n):
                    weigh(n - 1, (q - 1) % DEPTH)
                if s is not None and q == 3:
                    add_shared(s)

            def add_shared(s):
                dve.wait_ge(sy_ps, s + 1)
                x = X1[:, bass.ds(s * (BLK // P), BLK // P), :].rearrange("p t d -> p (t d)")
                T(x, ps_sy[:, 0:BLK], x, ALU.add).then_inc(sum_sb, 1)

            def block_rows(n):
                return wrow[:, bass.ds(n, 1), :, :].rearrange("p o j c -> p (o j) c")

            def low(n, q):
                v = q % 2
                dve.wait_ge(xt_hi_sb, n + 1)
                reused(dve, h_ps, n, 2)
                T(xt_lo[v], ps_t[v][:, 0:BLK], xt_hi[v].bitcast(F32), ALU.subtract).then_inc(xt_lo_sb, 1)
                dve.wait_ge(xs_in[q], slot_count(n, q, DEPTH))
                dve.tensor_copy(block_rows(n), xs[q][:, :, P:ROW]).then_inc(wrow_sb, 1)

            def weigh(n, q):
                dve.wait_ge(wrow_sb, n + 1)
                free_slot(dve, y_out[q], n, q, 2, DEPTH)
                dve.tensor_copy(yidx[q][:, :], block_rows(n)[:, :, 1])
                dve.wait_ge(y_ps, n + 1)
                T(yo[q], ps_y[q % 2][:, 0:BLK].rearrange("p (j d) -> p j d", d=P),
                  block_rows(n)[:, :, 0:1].to_broadcast([P, 2, P]), ALU.mult).then_inc(y_sb, 1)

            with dve.Fori(0, EARLY) as s:
                add_shared(s)
            low(0, 0)
            blocks(dve, step)
            weigh(NBLK - 1, (NBLK - 1) % DEPTH)

            dve.wait_ge(sum_sb, NU)

            for q in range(NG // QG):
                v = q % 2
                for r in range(QG):
                    g = q * QG + r
                    dve.wait_ge(ysum_sb, g + 1)
                    T(total[g], total[g], yb[g][:, :, 1, :], ALU.add).then_inc(total_sb, 1)
                    dve.wait_ge(total_sb, g + 1)
                    for t in range(TPG):
                        last = dve.bn_stats(st2[:, r * TPG + t, :], total[g][:, t, :])
                last.then_inc(stats2, 1)
                dve.wait_ge(stats2, q + 1)
                moments(moment2, q, st2, mt2, mean2, veps2)
                reused(dve, out_sb, q, 2, QG)
                reciprocal_root(rsqrt2, q, veps2[:, :], rsq2, rstd2[v][:, :])
                dve.scalar_tensor_tensor(out=nbias2[v][:, :], in0=mean2[:, :], scalar=-1.0, in1=rstd2[v][:, :],
                                         op0=ALU.mult, op1=ALU.mult).then_inc(norm2, 1)


_INS = ['L0_attn_u', 'L0_attn_a_params', 'L0_attn_B_w', 'L0_attn_C_w', 'L0_attn_D', 'L0_ffn_router_w', 'L0_ffn_router_b',
        'L0_ffn_sw1', 'L0_ffn_sb1', 'L0_ffn_sw2', 'L0_ffn_sb2', 'L0_ffn_rw1', 'L0_ffn_rb1', 'L0_ffn_rw2', 'L0_ffn_rb2']
_OUTS = [((NSEQ, SEQ, P), 'float32')]


def kernel(**inputs):
    import numpy as _np
    import concourse.bacc as _bacc
    from concourse import mybir as _mybir
    from concourse.bass_utils import run_bass_kernel_spmd as _run

    nc = _bacc.Bacc("TRN2", target_bir_lowering=False, num_devices=1)
    arrays, args = {}, []
    consts, pads, _ = shape_constants()
    for name, a in [("consts", consts), ("pads", pads)] + [(n, inputs[n]) for n in _INS]:
        a = _np.ascontiguousarray(a)
        arrays[f"in_{name}_dram"] = a
        args.append(nc.dram_tensor(f"in_{name}_dram", a.shape, _mybir.dt.from_np(a.dtype), kind="ExternalInput").ap())
    for i, (shape, dtype) in enumerate(_OUTS):
        dt = _mybir.dt.from_np(_np.dtype(dtype))
        args.append(nc.dram_tensor(f"out_{i}_dram", shape, dt, kind="ExternalOutput").ap())
    build(nc, *args)
    r = _run(nc, [arrays], core_ids=[0])
    got = tuple(r.results[0][f"out_{i}_dram"] for i in range(len(_OUTS)))
    return got[0]
```

```python
from contextlib import ExitStack
from itertools import islice

import numpy as np

import concourse.bass as bass
from concourse import mybir

F32 = mybir.dt.float32
F32R = mybir.dt.float32r
BF16 = mybir.dt.bfloat16
I32 = mybir.dt.int32
U32 = mybir.dt.uint32
ALU = mybir.AluOpType
ACT = mybir.ActivationFunctionType
AX = mybir.AxisListType.X

P = 128
SEQ = 256
NSEQ = 32
GT = 512
NG = NSEQ * SEQ // GT
TPG = GT // P
SPG = GT // SEQ
E = 8
EBITS = 3
K = 2
BLK = 256
NBLK = NG * GT * K // BLK + E
CAP = NG * GT + BLK
NULLS = NBLK - NG * GT * K // BLK
ROW = P + 2
NU = NG * GT // BLK
DEPTH = 4
UNITS_BETWEEN = 4
EARLY = NU // 2
HB = 2
HID = HB * P
B2 = 2 * HID + HB * P
B1 = B2 + P
WROW = B1 + HB
PT = 2 * TPG
QG = 4
QT = QG * TPG
POOL_SUMS = range(QG - 1, NG, QG)
POOL_NORMS = range(NG - QG - 2, NG - QG)
DVE_NORMS = range(NG - QG + 1, NG - 1)
SMALL, BIG = 8, 6 + E + 1
W_DONE = 4
TAB = 10 + 8 * 5
ROUTE_HALF = 9
MOMENTS, RSQRT, ROUTE, SLOT = 3, 11, 15, 2
EPS = 1e-5
PEEL = 8
LAST = 14


def shape_constants():
    n = np.arange(P)
    p = np.arange(P)
    k = np.where(p <= 64, p, p - 64)
    im = p > 64
    edge = (p == 0) | (p == 64)
    ang = 2 * np.pi * np.outer(n, k) / P
    cos, sin = np.cos(ang), np.sin(ang)
    sin[:, edge] = 0
    to_basis = np.where(im, -sin, cos)
    to_turned = np.where(im, -cos, -sin)
    to_turned[:, edge] = 0
    m = np.where(edge, 1.0, 2.0)
    from_basis = np.where(im, -sin, cos) * m / P
    from_turned = np.where(im, -cos, -sin) * m / P
    from_turned[:, edge] = 0
    omega = np.zeros((P, P))
    omega[:63] = -2 * np.sin(2 * np.pi * np.outer(np.arange(1, 64), k) / P)
    omega[:, edge] = 0
    key = np.tile(E - np.arange(E), (P, 1))
    before = np.triu(np.ones((P, P)), 1)
    start = np.tile(np.arange(E) * CAP, (P, 1))
    blocks = np.tile(np.arange(NBLK), (P, 1))
    meta = np.zeros((P, NG * TPG, K, 2))
    meta[..., 1] = ((np.arange(NG * TPG)[None, :] * P + n[:, None]) * K)[..., None] + np.arange(K)
    parts = {"to_basis": to_basis, "to_turned": to_turned, "from_basis": from_basis, "from_turned": from_turned,
             "ident": np.eye(P), "omega": omega, "before": before, "key": key, "start": start,
             "blocks": blocks, "meta": meta.reshape(P, -1)}
    where, at = {}, 0
    for name, part in parts.items():
        where[name] = (at, at + part.shape[1])
        at += part.shape[1]
    consts = np.concatenate(list(parts.values()), axis=1).astype(np.float32)
    pads = np.zeros(((E + NULLS) * BLK, ROW), np.float32)
    pads[:, P + 1] = NG * GT * K + np.arange(len(pads))
    return consts, pads, where


def build(nc, consts, pads, u, a_params, B_w, C_w, D, router_w, router_b, sw1, sb1, sw2, sb2, rw1, rb1, rw2, rb2, out):
    where = shape_constants()[2]
    NCONST = where["meta"][0]
    x_d = u.rearrange("b s d -> (b s) d").rearrange("(g t p) d -> g p t d", p=P, t=TPG)
    out_d = out.rearrange("b s d -> (b s) d").rearrange("(g t p) d -> g p t d", p=P, t=TPG)
    xs_d = nc.dram_tensor("slot_rows", (E * CAP + NULLS * BLK + 1, ROW), F32).ap()
    ys_d = nc.dram_tensor("results", (NG * GT * K + (E + NULLS) * BLK, P), F32).ap()
    y_d = ys_d[0:NG * GT * K, :].rearrange("(g t p k) d -> g p t (k d)", p=P, t=TPG, k=K)

    with ExitStack() as ctx:
        def sb(name, shape, dt=F32):
            return ctx.enter_context(nc.sbuf_tensor(name, shape, dt))

        def sem(name):
            return ctx.enter_context(nc.semaphore(name))

        def sems(name, n=2):
            return [sem(f"{name}{i}") for i in range(n)]

        bank = [ctx.enter_context(nc.psum_tensor(f"bank{i}", [P, 512], F32)) for i in range(8)]
        ps_xT, ps_b1, ps_b2, ps_x1T, ps_lg, ps_rank = bank[0], bank[1], bank[2], bank[3], bank[4], bank[7]
        ps_r = [bank[5], bank[6]]
        ps_t, ps_h, ps_y, ps_sh, ps_sy = bank[0:2], bank[2:4], (bank[4], bank[7]), bank[6], bank[5]

        cst = sb("cst", [P, NCONST])

        def const(name):
            return cst[:, where[name][0]:where[name][1]]

        ident = const("ident")
        bw = sb("bw", [P, P])
        cw = sb("cw", [P, P])
        cwT = sb("cwT", [P, P])
        apar = sb("apar", [64, 1])
        dcol = sb("dcol", [P, 1])
        rw = sb("rw", [P, E])
        rw_hi = sb("rw_hi", [P, E], F32R)
        rw_lo = sb("rw_lo", [P, E], F32R)
        rbias = sb("rbias", [P, E])
        g1T = sb("g1T", [P, P])
        g2T = sb("g2T", [P, P])
        m1T = sb("m1T", [P, P])
        m2T = sb("m2T", [P, P])
        skip = sb("skip", [P, P])
        lam = sb("lam", [P, 8])
        cosT = sb("cosT", [P, SEQ])
        sinT = sb("sinT", [P, SEQ])
        tmpT = sb("tmpT", [P, 2, SEQ // 2])
        before = sb("before", [P, P], BF16)
        allones = sb("allones", [P, P], BF16)

        wall = sb("wall", [P, E + 1, WROW])
        wshared = sb("wshared", [P, WROW], F32R)

        xg = [sb(f"xg{i}", [P, TPG, P]) for i in range(2)]
        uT = [sb(f"uT{i}", [P, GT]) for i in range(2)]
        scan = sb("scan", [P, 3 * GT])
        z1, z2, run = (scan[:, i * GT:(i + 1) * GT] for i in range(3))
        hh = [sb(f"hh{i}", [P, HB, GT]) for i in range(2)]
        hc = [hh[i][:, 0, :] for i in range(2)]
        hs = [hh[i][:, 1, :] for i in range(2)]
        x1b = [sb(f"x1b{i}", [P, TPG, P]) for i in range(2)]
        xr_hi = [sb(f"xr_hi{i}", [P, GT], F32R) for i in range(2)]
        xr_lo = [sb(f"xr_lo{i}", [P, GT], F32R) for i in range(2)]
        st = sb("st", [P, TPG, 6])
        mt = sb("mt", [P, 3, TPG])
        mean = sb("mean", [P, TPG])
        veps = sb("veps", [P, TPG])
        rsq = sb("rsq", [P, 3, TPG])
        rstd = [sb(f"rstd{i}", [P, TPG]) for i in range(2)]
        nbias = [sb(f"nbias{i}", [P, TPG]) for i in range(2)]
        lg = sb("lg", [P, PT, E])
        lgs = sb("lgs", [P, PT, E])
        ex = sb("ex", [P, PT, E])
        pr = sb("pr", [P, PT, E])
        pr2 = sb("pr2", [P, PT, E])
        hot = sb("hot", [P, K, PT, E])
        eq = sb("eq", [P, 2, PT, E])
        rc = sb("rc", [P, 8, PT])
        chosen = sb("chosen", [P, PT + 1, E], BF16)
        rank = sb("rank", [P, PT, E])
        hrank = sb("hrank", [P, K, PT, E])
        carry = sb("carry", [P, E])
        meta = sb("meta", [P, NG * TPG, K, 2])
        slots = sb("slots", [P, NG * TPG, K])
        pay = [sb(f"pay{i}", [P, TPG, K, ROW]) for i in range(2)]
        sidx = [sb(f"sidx{i}", [P, TPG, K], U32) for i in range(2)]

        X1 = sb("X1", [P, NG * TPG, P])
        b1r = X1[0:(E + 1) * HB, NG * TPG - 1, :]
        x1_hi = sb("x1_hi", [P, NG * GT], F32R)
        x1_lo = sb("x1_lo", [P, NG * GT], F32R)

        bt = sb("bt", [1, 6, E])
        bti = sb("bti", [1, E], I32)
        bcmp = scan[0:1, 0:2 * NBLK * E].rearrange("p (k n e) -> p k n e", k=2, e=E)
        bsum = sb("bsum", [1, 4, NBLK])
        btab = sb("btab", [1, NBLK], I32)
        pad_at = sb("pad_at", [1, E], I32)

        xs = [scan[:, i * 2 * ROW:(i + 1) * 2 * ROW].rearrange("p (j c) -> p j c", j=2) for i in range(DEPTH)]
        wb = [sb(f"wb{i}", [P, WROW], F32R)[:, :] for i in range(DEPTH)]
        xt_hi = [xr_hi[i][:, 0:BLK] for i in range(2)]
        xt_lo = [xr_lo[i][:, 0:BLK] for i in range(2)]
        hid = [hh[i][:, 0, :].rearrange("p (b n) -> p b n", b=HB) for i in range(2)]
        hid_s = [hh[i][:, 1, :].rearrange("p (b n) -> p b n", b=HB) for i in range(2)]
        yo = [xg[i // 2][:, i % 2 * 2:i % 2 * 2 + 2, :] for i in range(DEPTH)]
        yidx = [sb(f"yidx{i}", [P, 2], U32) for i in range(DEPTH)]
        wrow = pay[0][:, :, :, :].rearrange("p t k c -> p (t k c)")[:, 0:NBLK * 4].rearrange("p (n j c) -> p n j c", j=2, c=2)

        yb = [(x1_hi, x1_lo)[g // (NG // 2)][:, bass.ts(g % (NG // 2), TPG * K * P)].bitcast(F32)
              .rearrange("p (t k d) -> p t k d", k=K, d=P) for g in range(NG)]
        total = [X1[:, g * TPG:(g + 1) * TPG, :] for g in range(NG)]
        st2 = [cosT[:, i * QT * 6:(i + 1) * QT * 6].rearrange("p (t c) -> p t c", c=6) for i in range(2)]
        mt2 = sinT[:, 0:3 * QT].rearrange("p (c t) -> p c t", c=3)
        rsq2 = sinT[:, 3 * QT:6 * QT].rearrange("p (c t) -> p c t", c=3)
        mean2, veps2 = sinT[:, 6 * QT:7 * QT], sinT[:, 7 * QT:8 * QT]
        rstd2 = [sb(f"rstd2_{i}", [P, QT]) for i in range(2)]
        nbias2 = [sb(f"nbias2_{i}", [P, QT]) for i in range(2)]

        small_in, w_in, null_in = sem("small_in"), sem("w_in"), sem("null_in")
        x_in, x1_kept, hi_kept, lo_kept = sems("x_in"), sems("x1_kept"), sems("hi_kept"), sems("lo_kept")
        scattered = sems("scattered")
        set_pe, set_act, set_dve, w_parts, tab = (
            sem(n) for n in ("set_pe", "set_act", "set_dve", "w_parts", "tab"))
        xT_ps, uT_sb, b_ps, z_sb, run_sb, rot_sb, r_ps = (
            sem(n) for n in ("xT_ps", "uT_sb", "b_ps", "z_sb", "run_sb", "rot_sb", "r_ps"))
        stats, moment, rsqrt, rstd_sb, x1_sb, x1T_ps, hi_sb, lo_sb = (
            sem(n) for n in ("stats", "moment", "rsqrt", "rstd_sb", "x1_sb", "x1T_ps", "hi_sb", "lo_sb"))
        lg_ps, lg_sb, lmax, lgs_sb, ex_sb, route, rank_ps, rank_sb, slot_step, slot_sb, pay_sb = (
            sem(n) for n in ("lg_ps", "lg_sb", "lmax", "lgs_sb", "ex_sb", "route", "rank_ps", "rank_sb",
                             "slot_step", "slot_sb", "pay_sb"))
        table, pads_in, shared_in = sem("table"), sem("pads_in"), sem("shared_in")
        xs_in, wb_in = sems("xs_in", DEPTH), sems("wb_in", DEPTH)
        xsT_ps, xt_hi_sb, xt_lo_sb, h_ps, h_sb, y_ps, y_sb, wrow_sb = (
            sem(n) for n in ("xsT_ps", "xt_hi_sb", "xt_lo_sb", "h_ps", "h_sb", "y_ps", "y_sb", "wrow_sb"))
        y_out = sems("y_out", DEPTH)
        yb_sb, sh_ps, sh_sb, sy_ps, xb_sb, sum_sb = (sem(n) for n in ("yb_sb", "sh_ps", "sh_sb", "sy_ps", "xb_sb", "sum_sb"))
        yb_in = sems("yb_in", NG)
        ysum_sb, total_sb, stats2, moment2, rsqrt2, norm2, out_sb, out_done, out_pool, out_dve, pool_total = (
            sem(n) for n in ("ysum_sb", "total_sb", "stats2", "moment2", "rsqrt2", "norm2", "out_sb", "out_done", "out_pool", "out_dve", "pool_total"))

        keep_go, fetch_go, scatter_go, put_go = (sem(n) for n in ("keep_go", "fetch_go", "scatter_go", "put_go"))

        block = ctx.enter_context(nc.Block())

        def pipeline(eng, step, end=NG + 6):
            for i in range(-1, PEEL):
                step(i, i % 2)
            with eng.Fori(PEEL, LAST - 1, 2) as i:
                step(i, 0)
                step(i + 1, 1)
            for i in range(LAST, end):
                step(i, i % 2)

        def is_first(g, n=1):
            return isinstance(g, int) and g < n

        def group(i, lag):
            g = i - lag
            return g if not isinstance(g, int) or 0 <= g < NG else None

        def reused(eng, s, g, depth, each=1):
            if not is_first(g, depth):
                eng.wait_ge(s, (g - (depth - 1)) * each)

        def slot_count(g, v, depth=2):
            return (g - v) * (16 // depth) + 16

        def free_slot(eng, s, g, v, each=1, depth=2):
            if not is_first(g, depth):
                eng.wait_ge(s, slot_count(g - depth, v, depth) * each)

        def w1_part(w, low, b):
            return w[:, low * HID + b * P:low * HID + (b + 1) * P]

        def w2_block(w, b):
            return w[:, 2 * HID + b * P:2 * HID + (b + 1) * P].bitcast(F32)

        def bias2(w):
            return w[:, B2:B2 + P].bitcast(F32).unsqueeze(1).to_broadcast([P, BLK // P, P])

        def bias1(w, b):
            return w[:, B1 + b:B1 + b + 1].bitcast(F32)

        def blocks(eng, step):
            for n in range(2 * DEPTH):
                step(n, n % DEPTH, EARLY + n // DEPTH)
            with eng.Fori(2, NU - EARLY) as k:
                for q in range(DEPTH):
                    step(k * DEPTH + q, q, k + EARLY)
            for n in range(DEPTH * (NU - EARLY), NBLK):
                step(n, n % DEPTH, None)

        def normalise(eng, g):
            v = g // QG % 2
            for t in range(TPG):
                x, c = total[g][:, t, :], slice(g % QG * TPG + t, g % QG * TPG + t + 1)
                last = eng.tensor_scalar(x, x, rstd2[v][:, c], nbias2[v][:, c], ALU.mult, ALU.add)
            return last

        def block_word(eng, n):
            return eng.value_load(btab[0:1, bass.ds(n, 1)], min_val=0, max_val=((E * CAP + (NULLS - 1) * BLK) << EBITS) + E - 1)

        def fetch_rows(eng, word, n, q):
            reused(eng, xsT_ps, n, DEPTH)
            reused(eng, wrow_sb, n, DEPTH)
            eng.sem_inc(fetch_go, 1)
            eng.dma_start(xs[q], xs_d[bass.ds(word >> EBITS, BLK), :].rearrange("(j p) c -> p j c", p=P)).then_inc(xs_in[q], 16)

        def early_units(eng, unit, first, last):
            with eng.Fori(first, last - 1, 2) as s:
                unit(s, 0)
                unit(s + 1, 1)

        @block.sync
        def _(sp):
            small = [(cst[:, :], consts[:, 0:NCONST]), (bw[:, :], B_w), (cw[:, :], C_w),
                     (apar[:, :], a_params.rearrange("(p o) -> p o", o=1)),
                     (dcol[:, :], D.rearrange("(p o) -> p o", o=1)),
                     (rw[:, :], router_w), (rbias[:, :], router_b.partition_broadcast(P)),
                     (meta[:, :, :, :].rearrange("p t k c -> p (t k c)"), consts[:, NCONST:])]
            assert len(small) == SMALL
            for dst, src in small:
                sp.dma_start(dst, src).then_inc(small_in, 16)
            for g in range(2):
                sp.dma_start(xg[g][:, :, :], x_d[g]).then_inc(x_in[g], 16)
            big = [(wall[:, 0:E, HID:2 * HID], rw1.rearrange("e d h -> d e h")), (wall[:, E, HID:2 * HID], sw1),
                   (b1r[0:E * HB, :], rb1.rearrange("e (b h) -> (e b) h", b=HB)),
                   (b1r[E * HB:, :], sb1.rearrange("(b h) -> b h", b=HB)),
                   (wall[:, 0:E, B2:B2 + P], rb2.partition_broadcast(P)), (wall[:, E, B2:B2 + P], sb2.partition_broadcast(P))]
            for e in range(E + 1):
                src = sw2 if e == E else rw2[e]
                big.append((wall[:, e, 2 * HID:2 * HID + HB * P].rearrange("p (b d) -> p b d", b=HB),
                            src.rearrange("(b h) d -> h b d", b=HB)))
            assert len(big) == BIG
            for dst, src in big:
                sp.dma_start(dst, src).then_inc(w_in, 16)
            sp.dma_start(xs_d[E * CAP:E * CAP + NULLS * BLK, :], pads[E * BLK:, :]).then_inc(null_in, 16)

            def step(i, v):
                g = group(i, -2)
                if g is not None and not is_first(g, 2):
                    sp.wait_ge(xT_ps, g - 1)
                    sp.dma_start(xg[v][:, :, :], x_d[bass.ds(g, 1)].rearrange("o p t d -> (o p) t d")).then_inc(x_in[v], 16)
                g = group(i, 2)
                if g is not None:
                    sp.wait_ge(x1_sb, g + 1)
                    if isinstance(g, int) and g == PEEL - 3:
                        sp.wait_ge(set_pe, 4)
                    sp.dma_start(X1[:, bass.ds(g * TPG, TPG), :], x1b[v][:, :, :]).then_inc(x1_kept[v], 16)
                g = group(i, 3)
                if g is not None:
                    w = 1 - v
                    sp.wait_ge(hi_sb, g + 1)
                    sp.dma_start(x1_hi[:, bass.ds(g * GT, GT)].bitcast(F32), xr_hi[w][:, :].bitcast(F32)).then_inc(hi_kept[w], 16)
                    sp.wait_ge(lo_sb, g + 1)
                    sp.sem_inc(keep_go, 1)
                    sp.dma_start(x1_lo[:, bass.ds(g * GT, GT)].bitcast(F32), xr_lo[w][:, :].bitcast(F32)).then_inc(lo_kept[w], 16)

            pipeline(sp, step)

            sp.wait_ge(w_parts, W_DONE)
            sp.dma_start(wshared[:, :].bitcast(F32), wall[:, E, :]).then_inc(shared_in, 16)
            sp.wait_ge(table, 1)
            for e in range(E):
                at = sp.value_load(pad_at[0:1, e:e + 1], min_val=e * CAP, max_val=(e + 1) * CAP - BLK)
                sp.dma_start(xs_d[bass.ds(at, BLK), :], pads[e * BLK:(e + 1) * BLK, :]).then_inc(pads_in, 16)
            sp.wait_ge(table, 2)

            def fetch_weights(n, q):
                word = block_word(sp, n)
                reused(sp, yb_sb, n, DEPTH)
                sp.sem_inc(fetch_go, 1)
                sp.dma_start(wb[q].bitcast(F32), wall[:, bass.ds(word & (E - 1), 1), :].rearrange("p o c -> p (o c)")).then_inc(wb_in[q], 16)

            for n in range(DEPTH):
                fetch_weights(n, n)
            for v in range(2):
                sp.wait_ge(scattered[v], TPG * K * NG * 8)
            sp.wait_ge(pads_in, E * 16)
            sp.wait_ge(null_in, 16)
            for n in range(DEPTH):
                fetch_rows(sp, block_word(sp, n), n, n)

            def fetch(n, q, s):
                if q % 2 and not is_first(n + 1, DEPTH) and not (isinstance(n, int) and n + 1 >= NBLK):
                    fetch_rows(sp, block_word(sp, n + 1), n + 1, (q + 1) % DEPTH)
                if not is_first(n, DEPTH):
                    fetch_weights(n, q)

            blocks(sp, fetch)

            for q in range(DEPTH):
                sp.wait_ge(y_out[q], 2 * NBLK * 16 // DEPTH)

            for g in range(NG):
                sp.dma_start(yb[g].rearrange("p t k d -> p t (k d)"), y_d[g]).then_inc(yb_in[g], 16)
            for g in range(NG):
                if g in POOL_NORMS:
                    sp.wait_ge(out_pool, g - POOL_NORMS[0] + 1)
                elif g in DVE_NORMS:
                    sp.wait_ge(out_dve, g - DVE_NORMS[0] + 1)
                else:
                    sp.wait_ge(out_sb, sum(k not in POOL_NORMS and k not in DVE_NORMS for k in range(g + 1)))
                sp.dma_start(out_d[g], total[g]).then_inc(out_done, 16)
            sp.wait_ge(out_done, NG * 16)

        @block.tensor
        def _(pe):
            mm = pe.matmul
            pe.wait_ge(small_in, SMALL * 16)
            mm(ps_b1[:, 0:1], const("omega")[0:63, :], apar[0:63, :], start=True, stop=True).then_inc(set_pe, 1)
            mm(ps_b2[:, 0:P], bw[:, :], const("to_basis"), start=True, stop=True)
            mm(ps_b2[:, P:2 * P], bw[:, :], const("to_turned"), start=True, stop=True)
            pe.transpose(ps_b2[:, 2 * P:3 * P], cw[:, :], ident).then_inc(set_pe, 1)
            pe.wait_ge(set_act, 1)
            mm(ps_x1T[:, 0:P], const("from_basis"), cwT[:, :], start=True, stop=True)
            mm(ps_x1T[:, P:2 * P], const("from_turned"), cwT[:, :], start=True, stop=True).then_inc(set_pe, 1)
            pe.wait_ge(w_in, BIG * 16)
            pe.transpose(ps_lg[:, 0:(E + 1) * HB], b1r[:, :], ident[0:(E + 1) * HB, 0:(E + 1) * HB]).then_inc(set_pe, 1)

            def step(i, v):
                w = 1 - v
                g = group(i, 0)
                if g is not None:
                    pe.wait_ge(uT_sb, g + 1)
                    if is_first(g):
                        pe.wait_ge(set_act, 2)
                        pe.wait_ge(tab, 2)
                    reused(pe, z_sb, g, 1)
                    mm(ps_b1[:, :], g1T[:, :], uT[v][:, :], start=True, stop=True)
                    mm(ps_b2[:, :], g2T[:, :], uT[v][:, :], start=True, stop=True).then_inc(b_ps, 1)
                g = group(i, 1)
                if g is not None:
                    pe.wait_ge(rot_sb, g + 1)
                    if is_first(g):
                        pe.wait_ge(set_act, 3)
                        pe.wait_ge(set_dve, 1)
                    reused(pe, x1_sb, g, 2)
                    for t in range(TPG):
                        c = slice(t * P, (t + 1) * P)
                        mm(ps_r[w][:, c], hc[w][:, c], m1T[:, :], start=True, stop=False)
                        mm(ps_r[w][:, c], hs[w][:, c], m2T[:, :], start=False, stop=False)
                        last = mm(ps_r[w][:, c], uT[w][:, c], skip[:, :], start=False, stop=True)
                    last.then_inc(r_ps, 1)
                g = group(i, -1)
                if g is not None:
                    pe.wait_ge(x_in[w], slot_count(g, w))
                    reused(pe, uT_sb, g, 1)
                    for t in range(TPG):
                        last = pe.transpose(ps_xT[:, t * P:(t + 1) * P], xg[w][:, t, :], ident)
                    last.then_inc(xT_ps, 1)
                g = group(i, 6) if v == 0 else None
                if g is not None:
                    pe.wait_ge(route, (g + 2) * ROUTE)
                    reused(pe, rank_sb, g, 1)
                    mm(ps_rank[:, 0:(PT + 1) * E], before[:, :], chosen[:, :, :].rearrange("p t e -> p (t e)"), start=True, stop=False)
                    for t in range(PT):
                        last = mm(ps_rank[:, (t + 1) * E:(PT + 1) * E].rearrange("p (t e) -> p t e", e=E), allones[:, :],
                                  chosen[:, t, :].unsqueeze(1).to_broadcast([P, PT - t, E]), start=False, stop=t == PT - 1)
                    last.then_inc(rank_ps, 2)
                g = group(i, 3)
                if g is not None:
                    pe.wait_ge(hi_sb, g + 1)
                    pe.wait_ge(lo_sb, g + 1)
                    if is_first(g):
                        pe.wait_ge(set_act, 4)
                        pe.wait_ge(w_parts, 2)
                    if w == 0 and not is_first(g, 2):
                        pe.wait_ge(lg_sb, g)
                    for t in range(TPG):
                        c = slice(t * P, (t + 1) * P)
                        o = ps_lg[:, (w * TPG + t) * E:(w * TPG + t + 1) * E]
                        mm(o, xr_hi[w][:, c], rw_hi[:, :], start=True, stop=False)
                        mm(o, xr_hi[w][:, c], rw_lo[:, :], start=False, stop=False)
                        last = mm(o, xr_lo[w][:, c], rw_hi[:, :], start=False, stop=True)
                    last.then_inc(lg_ps, 1)
                g = group(i, 2)
                if g is not None:
                    pe.wait_ge(x1_sb, g + 1)
                    if is_first(g):
                        pe.wait_ge(set_act, 3)
                    reused(pe, lo_sb, g, 1)
                    reused(pe, hi_sb, g, 1)
                    for t in range(TPG):
                        last = pe.transpose(ps_x1T[:, t * P:(t + 1) * P], x1b[v][:, t, :], ident)
                    last.then_inc(x1T_ps, 1)

            pipeline(pe, step)

            for s in (uT_sb, z_sb, x1_sb, hi_sb, lo_sb):
                pe.wait_ge(s, NG)
            for v in range(2):
                pe.wait_ge(hi_kept[v], NG * 8)
                pe.wait_ge(lo_kept[v], NG * 8)
            pe.wait_ge(shared_in, 16)

            def split3(o, w, b, xh, xl):
                mm(o, w1_part(w, 0, b), xh, start=True, stop=False)
                mm(o, w1_part(w, 1, b), xh, start=False, stop=False)
                return mm(o, w1_part(w, 0, b), xl, start=False, stop=True)

            def second(ps, h, w):
                for j in range(BLK // P):
                    o = ps[:, j * P:(j + 1) * P]
                    for b in range(HB):
                        last = mm(o, h[:, b, j * P:(j + 1) * P], w2_block(w, b), start=b == 0, stop=b == HB - 1)
                return last

            def turn(n, q):
                pe.wait_ge(xs_in[q], slot_count(n, q, DEPTH))
                reused(pe, xt_hi_sb, n, 2)
                reused(pe, xt_lo_sb, n, 2)
                for j in range(2):
                    last = pe.transpose(ps_t[q % 2][:, j * P:(j + 1) * P], xs[q][:, j, 0:P], ident)
                last.then_inc(xsT_ps, 1)

            def first_layer(n, q):
                v = q % 2
                pe.wait_ge(wb_in[q], slot_count(n, q, DEPTH))
                pe.wait_ge(xt_hi_sb, n + 1)
                pe.wait_ge(xt_lo_sb, n + 1)
                reused(pe, h_sb, n, 2)
                for b in range(HB):
                    last = split3(ps_h[v][:, b * BLK:(b + 1) * BLK], wb[q], b, xt_hi[v], xt_lo[v])
                last.then_inc(h_ps, 1)

            def second_layer(n, q):
                pe.wait_ge(h_sb, n + 1)
                reused(pe, y_sb, n, 2)
                second(ps_y[q % 2], hid[q % 2], wb[q]).then_inc(y_ps, 1)

            def shared_first(s):
                reused(pe, sh_sb, s, 1)
                c = bass.ds(s * BLK, BLK)
                for b in range(HB):
                    last = split3(ps_sh[:, b * BLK:(b + 1) * BLK], wshared[:, :], b, x1_hi[:, c], x1_lo[:, c])
                last.then_inc(sh_ps, 1)

            def shared_second(s, v=0):
                pe.wait_ge(sh_sb, s + 1)
                reused(pe, sum_sb, s, 1)
                second(ps_sy, hid_s[v], wshared[:, :]).then_inc(sy_ps, 1)

            def early(s, v):
                shared_first(s)
                shared_second(s - 1, 1 - v)

            def step(n, q, s):
                if not isinstance(n, int) or n + 1 < NBLK:
                    turn(n + 1, (q + 1) % DEPTH)
                first_layer(n, q)
                if not is_first(n):
                    second_layer(n - 1, (q - 1) % DEPTH)
                if s is not None and q == 0:
                    shared_first(s)
                if s is not None and q == 3:
                    shared_second(s)

            shared_first(0)
            shared_first(1)
            shared_second(0)
            early_units(pe, early, 2, EARLY)
            shared_second(EARLY - 1, 1)
            pe.wait_ge(lg_sb, NG)
            pe.wait_ge(rank_sb, NG)
            turn(0, 0)
            blocks(pe, step)
            second_layer(NBLK - 1, (NBLK - 1) % DEPTH)

        @block.gpsimd
        def _(pool):
            pool.wait_ge(small_in, SMALL * 16)
            pool.tensor_copy(rw_hi[:, :], rw[:, :]).then_inc(w_parts, 1)
            pool.wait_ge(w_parts, 1)
            pool.tensor_tensor(rw_lo[:, :], rw[:, :], rw_hi[:, :].bitcast(F32), ALU.subtract).then_inc(w_parts, 1)
            pool.wait_ge(w_in, BIG * 16)
            pool.tensor_copy(wall[:, :, 0:HID].bitcast(F32R), wall[:, :, HID:2 * HID]).then_inc(w_parts, 1)
            pool.wait_ge(w_parts, 3)
            lo = wall[:, :, HID:2 * HID]
            pool.tensor_tensor(lo.bitcast(F32R), lo, wall[:, :, 0:HID], ALU.subtract).then_inc(w_parts, 1)

            def scatter(g, v):
                pool.wait_ge(pay_sb, g + 1)
                pool.sem_inc(scatter_go, 1)
                for t in range(TPG):
                    for k in range(K):
                        pool.indirect_dma_start(xs_d, bass.IndirectOffsetOnAxis(ap=sidx[v][:, t, k:k + 1], axis=0),
                                                pay[v][:, t, k, :], None).then_inc(scattered[v], 16)

            with pool.Fori(0, NG - 1, 2) as g:
                scatter(g, 0)
                scatter(g + 1, 1)

            def put(n, q):
                pool.wait_ge(y_sb, n + 1)
                pool.sem_inc(put_go, 1)
                for j in range(2):
                    pool.indirect_dma_start(ys_d, bass.IndirectOffsetOnAxis(ap=yidx[q][:, j:j + 1], axis=0),
                                            yo[q][:, j, :], None).then_inc(y_out[q], 16)

            with pool.Fori(0, NBLK // DEPTH) as k:
                for q in range(DEPTH):
                    put(k * DEPTH + q, q)

            pool.wait_ge(sum_sb, NU)
            for g in range(NG):
                pool.wait_ge(yb_in[g], 16)
                pool.tensor_tensor(total[g], total[g], yb[g][:, :, 0, :], ALU.add).then_inc(ysum_sb, 1)
                if g in POOL_SUMS:
                    pool.wait_ge(ysum_sb, g + 1)
                    pool.tensor_tensor(total[g], total[g], yb[g][:, :, 1, :], ALU.add).then_inc(pool_total, 1)
            pool.wait_ge(norm2, POOL_NORMS[0] // QG + 1)
            for g in POOL_NORMS:
                normalise(pool, g).then_inc(out_pool, 1)

        @block.scalar
        def _(act):
            act.wait_ge(set_pe, 2)
            act.copy(cwT[:, :], ps_b2[:, 2 * P:3 * P]).then_inc(set_act, 1)
            act.copy(g1T[:, :], ps_b2[:, 0:P])
            act.copy(g2T[:, :], ps_b2[:, P:2 * P]).then_inc(set_act, 1)
            act.wait_ge(set_pe, 3)
            act.copy(m1T[:, :], ps_x1T[:, 0:P])
            act.copy(m2T[:, :], ps_x1T[:, P:2 * P]).then_inc(set_act, 1)
            act.wait_ge(set_pe, 4)
            act.copy(wall[:, :, B1:B1 + HB], ps_lg[:, 0:(E + 1) * HB].rearrange("p (e b) -> p e b", b=HB)).then_inc(set_act, 1)

            def step(i, v):
                w = 1 - v
                g = group(i, -1)
                if g is not None:
                    act.wait_ge(xT_ps, g + 1)
                    reused(act, r_ps, g, 2)
                    act.copy(uT[w][:, :], ps_xT[:, :]).then_inc(uT_sb, 1)
                g = group(i, 2)
                if g is not None:
                    act.wait_ge(x1T_ps, g + 1)
                    reused(act, lg_ps, g, 2)
                    free_slot(act, hi_kept[v], g, v)
                    act.copy(xr_hi[v][:, :], ps_x1T[:, :]).then_inc(hi_sb, 1)
                g = group(i, 6)
                if g is not None:
                    act.wait_ge(slot_sb, g + (2 - v))
                    act.wait_ge(x1_kept[v], slot_count(g, v))
                    free_slot(act, scattered[v], g, v, TPG * K)
                    c = bass.ds(g * TPG, TPG)
                    act.copy(pay[v][:, :, :, 0:P], X1[:, c, :].unsqueeze(2).to_broadcast([P, TPG, K, P]))
                    act.copy(pay[v][:, :, :, P:ROW], meta[:, c, :, :])
                    act.copy(sidx[v][:, :, :], slots[:, c, :]).then_inc(pay_sb, 1)
                g = group(i, 4) if v == 0 else None
                if g is not None:
                    act.wait_ge(lgs_sb, g + 2)
                    if not is_first(g, 2):
                        act.wait_ge(route, g * ROUTE)
                    act.activation(ex[:, :, :], lgs[:, :, :], ACT.Exp).then_inc(ex_sb, 2)
                g = group(i, 1)
                if g is not None:
                    act.wait_ge(rstd_sb, g + 1)
                    reused(act, x1T_ps, g, 2)
                    free_slot(act, x1_kept[w], g, w)
                    for t in range(TPG):
                        last = act.activation(x1b[w][:, t, :], ps_r[w][:, t * P:(t + 1) * P], ACT.Identity,
                                              bias=nbias[w][:, t:t + 1], scale=rstd[w][:, t:t + 1])
                    last.then_inc(x1_sb, 1)

            def shared_hidden(s, v=0):
                act.wait_ge(sh_ps, s + 1)
                reused(act, sy_ps, s, 2)
                for b in range(HB):
                    last = act.activation(hid_s[v][:, b, :], ps_sh[:, b * BLK:(b + 1) * BLK], ACT.Gelu, bias=bias1(wshared[:, :], b))
                last.then_inc(sh_sb, 1)

            pipeline(act, step, NG + 4)
            act.wait_ge(r_ps, NG)
            for i in range(NG + 4, NG + 6):
                for s in range(UNITS_BETWEEN * (i - NG - 4), UNITS_BETWEEN * (i - NG - 3)):
                    shared_hidden(s, s % 2)
                step(i, i % 2)
            early_units(act, shared_hidden, 2 * UNITS_BETWEEN, EARLY)
            act.wait_ge(lg_ps, NG)
            for v in range(2):
                act.wait_ge(hi_kept[v], NG * 8)

            def step(n, q, s):
                if not isinstance(n, int) or n + 1 < NBLK:
                    high(n + 1, (q + 1) % 2)
                ahead = n + DEPTH - 1
                if q % 2 == 0 and not is_first(ahead, DEPTH) and not (isinstance(ahead, int) and ahead >= NBLK):
                    fetch_rows(act, block_word(act, ahead), ahead, (q - 1) % DEPTH)
                hidden(n, q)
                if s is not None and q == 0:
                    act.wait_ge(sy_ps, s)
                    shared_hidden(s)

            def high(n, v):
                act.wait_ge(xsT_ps, n + 1)
                reused(act, h_ps, n, 2)
                act.copy(xt_hi[v], ps_t[v][:, 0:BLK]).then_inc(xt_hi_sb, 1)

            def hidden(n, q):
                v = q % 2
                act.wait_ge(h_ps, n + 1)
                reused(act, y_ps, n, 2)
                for b in range(HB):
                    last = act.activation(hid[v][:, b, :], ps_h[v][:, b * BLK:(b + 1) * BLK], ACT.Gelu, bias=bias1(wb[q], b))
                last.then_inc(h_sb, 1)

            high(0, 0)
            blocks(act, step)

            for g in range(NG):
                if g in POOL_NORMS or g in DVE_NORMS:
                    continue
                act.wait_ge(norm2, g // QG + 1)
                for t in range(TPG):
                    c = slice(g % QG * TPG + t, g % QG * TPG + t + 1)
                    x, v = total[g][:, t, :], g // QG % 2
                    last = act.activation(x, x, ACT.Identity, bias=nbias2[v][:, c], scale=rstd2[v][:, c])
                last.then_inc(out_sb, 1)

        @block.vector
        def _(dve):
            T = dve.tensor_tensor

            def linker(s, inc=1):
                n = [0]

                def link(base, ins):
                    n[0] += inc
                    ins.then_inc(s, inc)
                    dve.wait_ge(s, base + n[0])

                return link, n

            link, links = linker(tab)
            dve.wait_ge(small_in, SMALL * 16)
            link(0, dve.tensor_scalar(lam[:, 7:8], dcol[:, :], 1.0, None, ALU.add))
            dve.tensor_scalar(skip[:, :], ident, lam[:, 7:8], None, ALU.mult)
            dve.tensor_copy(before[:, :], const("before"))
            dve.memset(allones[:, :], 1.0)
            dve.memset(chosen[:, PT, :], 0.0)
            dve.tensor_copy(carry[:, :], const("start")).then_inc(set_dve, 1)
            dve.wait_ge(set_pe, 1)
            link(0, dve.tensor_copy(lam[:, 2:3], ps_b1[:, 0:1]))
            link(0, T(lam[:, 3:4], lam[:, 2:3], lam[:, 2:3], ALU.mult))
            link(0, dve.tensor_scalar(lam[:, 4:5], lam[:, 3:4], 1.0, None, ALU.add))
            link(0, dve.reciprocal(lam[:, 5:6], lam[:, 4:5]))
            link(0, dve.tensor_scalar(lam[:, 6:7], lam[:, 3:4], -1.0, 1.0, ALU.mult, ALU.add))
            link(0, T(lam[:, 0:1], lam[:, 6:7], lam[:, 5:6], ALU.mult))
            link(0, dve.tensor_scalar(lam[:, 6:7], lam[:, 2:3], -2.0, None, ALU.mult))
            link(0, T(lam[:, 1:2], lam[:, 6:7], lam[:, 5:6], ALU.mult))
            dve.memset(cosT[:, 0:1], 1.0)
            link(0, dve.memset(sinT[:, 0:1], 0.0))
            n = 1
            while n < SEQ:
                c, s = lam[:, 0:1], lam[:, 1:2]
                dve.tensor_scalar(tmpT[:, 0, 0:n], sinT[:, 0:n], s, None, ALU.mult)
                link(0, dve.tensor_scalar(tmpT[:, 1, 0:n], cosT[:, 0:n], s, None, ALU.mult))
                dve.scalar_tensor_tensor(out=cosT[:, n:2 * n], in0=cosT[:, 0:n], scalar=c, in1=tmpT[:, 0, 0:n],
                                         op0=ALU.mult, op1=ALU.subtract)
                link(0, dve.scalar_tensor_tensor(out=sinT[:, n:2 * n], in0=sinT[:, 0:n], scalar=c,
                                                 in1=tmpT[:, 1, 0:n], op0=ALU.mult, op1=ALU.add))
                T(lam[:, 2:3], s, s, ALU.mult)
                link(0, T(lam[:, 3:4], c, s, ALU.mult))
                link(0, dve.scalar_tensor_tensor(out=lam[:, 0:1], in0=c, scalar=c, in1=lam[:, 2:3],
                                                 op0=ALU.mult, op1=ALU.subtract))
                link(0, dve.tensor_scalar(lam[:, 1:2], lam[:, 3:4], 2.0, None, ALU.mult))
                n *= 2

            assert links[0] == TAB
            cos2 = cosT[:, :].unsqueeze(1).to_broadcast([P, SPG, SEQ])
            sin2 = sinT[:, :].unsqueeze(1).to_broadcast([P, SPG, SEQ])
            per_e = [P, PT, E]

            def seqs(a):
                return a.rearrange("p (s t) -> p s t", s=SPG)

            def linked(s, inc=1):
                n = [0]

                def link(base, ins):
                    n[0] += inc
                    ins.then_inc(s, inc)
                    yield
                    dve.wait_ge(s, base + n[0])

                return link, n

            def in_turns(*chains):
                chains = list(chains)
                while chains:
                    for c in list(chains):
                        if next(c, chains) is chains:
                            chains.remove(c)

            def moments(s, g, st, m, mean, veps):
                link, n = linked(s)
                base = g * MOMENTS
                me, mo, qe, qo = st[:, :, 1], st[:, :, 4], st[:, :, 2], st[:, :, 5]
                T(m[:, 0, :], me, mo, ALU.add)
                T(m[:, 1, :], me, mo, ALU.subtract)
                yield from link(base, T(m[:, 2, :], qe, qo, ALU.add))
                dve.tensor_scalar(mean[:, :], m[:, 0, :], 0.5, None, ALU.mult)
                dve.tensor_scalar(m[:, 2, :], m[:, 2, :], 1.0 / P, EPS, ALU.mult, ALU.add)
                yield from link(base, dve.scalar_tensor_tensor(out=m[:, 1, :], in0=m[:, 1, :], scalar=0.25, in1=m[:, 1, :],
                                                               op0=ALU.mult, op1=ALU.mult))
                yield from link(base, T(veps[:, :], m[:, 1, :], m[:, 2, :], ALU.add))
                assert n[0] == MOMENTS

            def reciprocal_root(s, g, x, t, y):
                link, n = linked(s)
                base = g * RSQRT
                yield from link(base, dve.tensor_scalar(t[:, 0, :].bitcast(I32), x.bitcast(I32), 1, None, ALU.logical_shift_right))
                yield from link(base, dve.tensor_scalar(t[:, 1, :].bitcast(I32), t[:, 0, :].bitcast(I32), -1.0, float(0x5F3759DF),
                                                        ALU.mult, ALU.add))
                for k in range(3):
                    yield from link(base, T(t[:, 0, :], t[:, 1, :], t[:, 1, :], ALU.mult))
                    yield from link(base, dve.scalar_tensor_tensor(out=t[:, 2, :], in0=t[:, 0, :], scalar=-0.5, in1=x,
                                                                   op0=ALU.mult, op1=ALU.mult))
                    o = y if k == 2 else t[:, 1, :]
                    yield from link(base, dve.scalar_tensor_tensor(out=o, in0=t[:, 2, :], scalar=1.5, in1=t[:, 1, :],
                                                                   op0=ALU.add, op1=ALU.mult))
                assert n[0] == RSQRT

            def turned(g, v):
                dve.wait_ge(b_ps, g + 1)
                T(seqs(z1), seqs(ps_b1[:, :]), cos2, ALU.mult)
                yield
                T(seqs(z2), seqs(ps_b2[:, :]), sin2, ALU.mult).then_inc(z_sb, 1)
                yield
                dve.wait_ge(z_sb, g + 1)
                for q in range(SPG):
                    c = slice(q * SEQ, (q + 1) * SEQ)
                    last = dve.tensor_tensor_scan(run[:, c], z1[:, c], z2[:, c], 0.0, op0=ALU.add, op1=ALU.add)
                last.then_inc(run_sb, 1)
                yield
                dve.wait_ge(run_sb, g + 1)
                reused(dve, r_ps, g, 2)
                T(seqs(hc[v]), seqs(run), cos2, ALU.mult)
                yield
                T(seqs(hs[v]), seqs(run), sin2, ALU.mult).then_inc(rot_sb, 1)
                yield

            def low_parts(g, v):
                dve.wait_ge(x1T_ps, g + 1)
                dve.wait_ge(hi_sb, g + 1)
                reused(dve, lg_ps, g, 2)
                free_slot(dve, lo_kept[v], g, v)
                T(xr_lo[v][:, :], ps_x1T[:, :], xr_hi[v][:, :].bitcast(F32), ALU.subtract).then_inc(lo_sb, 1)
                yield

            def norm(g, w):
                dve.wait_ge(r_ps, g + 1)
                for t in range(TPG):
                    last = dve.bn_stats(st[:, t, :], ps_r[w][:, t * P:(t + 1) * P])
                last.then_inc(stats, 1)
                yield
                dve.wait_ge(stats, g + 1)
                yield from moments(moment, g, st, mt, mean, veps)
                reused(dve, x1_sb, g, 2)
                yield from reciprocal_root(rsqrt, g, veps[:, :], rsq, rstd[w][:, :])
                dve.scalar_tensor_tensor(out=nbias[w][:, :], in0=mean[:, :], scalar=-1.0, in1=rstd[w][:, :],
                                         op0=ALU.mult, op1=ALU.mult).then_inc(rstd_sb, 1)

            def routed(g):
                dve.wait_ge(lg_ps, g + 2)
                T(lg[:, :, :], ps_lg[:, 0:PT * E].rearrange("p (t e) -> p t e", e=E),
                  rbias[:, :].unsqueeze(1).to_broadcast(per_e), ALU.add).then_inc(lg_sb, 2)
                yield
                dve.wait_ge(lg_sb, g + 2)
                dve.reduce_max(rc[:, 0, :], lg[:, :, :], AX).then_inc(lmax, 2)
                yield
                dve.wait_ge(lmax, g + 2)
                T(lgs[:, :, :], lg[:, :, :], rc[:, 0, :].unsqueeze(2).to_broadcast(per_e),
                  ALU.subtract).then_inc(lgs_sb, 2)
                yield
                dve.wait_ge(ex_sb, g + 2)
                link, n = linked(route, 2)
                base = g * ROUTE

                def over_e(a):
                    return a.unsqueeze(2).to_broadcast(per_e)

                keys = const("key").unsqueeze(1).to_broadcast(per_e)
                yield from link(base, dve.reduce_sum(rc[:, 1, :], ex[:, :, :], AX))
                yield from link(base, dve.reciprocal(rc[:, 2, :], rc[:, 1, :]))
                yield from link(base, T(pr[:, :, :], ex[:, :, :], over_e(rc[:, 2, :]), ALU.mult))

                def largest(p, top, best, mask):
                    yield from link(base, dve.reduce_max(top, p, AX))
                    yield from link(base, T(eq[:, 0, :, :], p, over_e(top), ALU.is_equal))
                    yield from link(base, T(eq[:, 1, :, :], eq[:, 0, :, :], keys, ALU.mult))
                    yield from link(base, dve.reduce_max(best, eq[:, 1, :, :], AX))
                    yield from link(base, T(mask, eq[:, 1, :, :], over_e(best), ALU.is_equal))

                yield from largest(pr[:, :, :], rc[:, 3, :], rc[:, 5, :], hot[:, 0, :, :])
                yield from link(base, dve.scalar_tensor_tensor(out=pr2[:, :, :], in0=hot[:, 0, :, :], scalar=-2.0, in1=pr[:, :, :],
                                                               op0=ALU.mult, op1=ALU.add))
                yield from largest(pr2[:, :, :], rc[:, 4, :], rc[:, 6, :], hot[:, 1, :, :])
                if not is_first(g, 2):
                    dve.wait_ge(rank_ps, g)
                dve.tensor_copy(meta[:, bass.ds(g * TPG, PT), :, 0].rearrange("p t k -> p k t"), rc[:, 3:5, :])
                yield from link(base, T(chosen[:, 0:PT, :], hot[:, 0, :, :], hot[:, 1, :, :], ALU.add))
                assert n[0] == 2 * ROUTE

            def slotted(g):
                dve.wait_ge(rank_ps, g + 2)
                link, n = linked(slot_step, 2)
                base = g * SLOT
                ps = ps_rank[:, 0:(PT + 1) * E].rearrange("p (t e) -> p t e", e=E)
                yield from link(base, T(rank[:, :, :], ps[:, 0:PT, :], carry[:, :].unsqueeze(1).to_broadcast(per_e), ALU.add))
                T(carry[:, :], ps[:, PT, :], carry[:, :], ALU.add).then_inc(rank_sb, 2)
                yield from link(base, T(hrank[:, :, :, :], hot[:, :, :, :], rank[:, :, :].unsqueeze(1).to_broadcast([P, K, PT, E]),
                                        ALU.mult))
                assert n[0] == 2 * SLOT
                dve.reduce_sum(slots[:, bass.ds(g * TPG, PT), :].rearrange("p t k -> p k t"), hrank[:, :, :, :], AX).then_inc(slot_sb, 2)
                yield

            def state(i, v):
                if group(i, 0) is not None:
                    yield from turned(group(i, 0), v)
                if group(i, 2) is not None:
                    yield from low_parts(group(i, 2), v)

            pair = [iter(())]

            def router(i, v):
                if v == 0 and group(i, 6) is not None:
                    yield from slotted(group(i, 6))
                if v == 0:
                    pair[0] = iter(()) if group(i, 4) is None else routed(group(i, 4))
                yield from islice(pair[0], ROUTE_HALF) if v == 0 else pair[0]

            def step(i, v):
                chains = [state(i, v)]
                if group(i, 1) is not None:
                    chains.append(norm(group(i, 1), 1 - v))
                chains.append(router(i, v))
                in_turns(*chains)

            pipeline(dve, step)

            link, n = linker(tab)
            base = TAB
            c, nb, upto, cnt = (bt[:, k, :] for k in range(4))
            dve.wait_ge(rank_sb, NG)
            dve.tensor_copy(pad_at[:, :], carry[0:1, :]).then_inc(table, 1)
            link(base, T(cnt, carry[0:1, :], const("start")[0:1, :], ALU.subtract))
            link(base, dve.tensor_scalar(bti[:, :], cnt, float(BLK - 1), None, ALU.add))
            link(base, dve.tensor_scalar(bti[:, :], bti[:, :], 8, None, ALU.logical_shift_right))
            link(base, dve.tensor_copy(nb, bti[:, :]))
            link(base, dve.memset(c, 0.0))
            link(base, dve.tensor_tensor_scan(upto, nb, c, 0.0, op0=ALU.add, op1=ALU.add))
            be = [1, NBLK, E]
            link(base, T(bcmp[:, 0, :, :], const("blocks")[0:1, :].unsqueeze(2).to_broadcast(be),
                         upto.unsqueeze(1).to_broadcast(be), ALU.is_ge))
            link(base, T(bcmp[:, 1, :, :], bcmp[:, 0, :, :], nb.unsqueeze(1).to_broadcast(be), ALU.mult))
            link(base, dve.reduce_sum(bsum[:, 0:2, :], bcmp[:, :, :, :], AX))
            link(base, T(bsum[:, 2, :], const("blocks")[0:1, :], bsum[:, 1, :], ALU.subtract))
            link(base, dve.tensor_scalar(bsum[:, 3, :], bsum[:, 0, :], float(CAP), None, ALU.mult))
            dve.tensor_scalar(bsum[:, 0, :], bsum[:, 0, :], float(E - 1), None, ALU.min)
            link(base, dve.scalar_tensor_tensor(out=bsum[:, 1, :], in0=bsum[:, 2, :], scalar=float(BLK), in1=bsum[:, 3, :],
                                                op0=ALU.mult, op1=ALU.add))
            dve.scalar_tensor_tensor(out=btab[:, :], in0=bsum[:, 1, :], scalar=float(1 << EBITS), in1=bsum[:, 0, :],
                                     op0=ALU.mult, op1=ALU.add).then_inc(table, 1)

            dve.wait_ge(shared_in, 16)
            for v in range(2):
                dve.wait_ge(x1_kept[v], NG * 8)
                dve.wait_ge(lo_kept[v], NG * 8)
            dve.wait_ge(lg_ps, NG)
            dve.wait_ge(xT_ps, NG)
            dve.wait_ge(pay_sb, EARLY * BLK // GT)

            def step(n, q, s):
                if not isinstance(n, int) or n + 1 < NBLK:
                    low(n + 1, (q + 1) % DEPTH)
                if not is_first(n):
                    weigh(n - 1, (q - 1) % DEPTH)
                if s is not None and q == 3:
                    add_shared(s)

            def add_shared(s):
                x = X1[:, bass.ds(s * (BLK // P), BLK // P), :]
                T(x, x, bias2(wshared[:, :]), ALU.add).then_inc(xb_sb, 1)
                dve.wait_ge(xb_sb, s + 1)
                dve.wait_ge(sy_ps, s + 1)
                T(x, ps_sy[:, 0:BLK].rearrange("p (j d) -> p j d", d=P), x, ALU.add).then_inc(sum_sb, 1)

            def block_rows(n):
                return wrow[:, bass.ds(n, 1), :, :].rearrange("p o j c -> p (o j) c")

            def low(n, q):
                v = q % 2
                dve.wait_ge(xt_hi_sb, n + 1)
                reused(dve, h_ps, n, 2)
                T(xt_lo[v], ps_t[v][:, 0:BLK], xt_hi[v].bitcast(F32), ALU.subtract).then_inc(xt_lo_sb, 1)
                dve.wait_ge(xs_in[q], slot_count(n, q, DEPTH))
                dve.tensor_copy(block_rows(n), xs[q][:, :, P:ROW]).then_inc(wrow_sb, 1)

            def weigh(n, q):
                dve.wait_ge(wrow_sb, n + 1)
                free_slot(dve, y_out[q], n, q, 2, DEPTH)
                dve.tensor_copy(yidx[q][:, :], block_rows(n)[:, :, 1])
                dve.wait_ge(y_ps, n + 1)
                T(yo[q], ps_y[q % 2][:, 0:BLK].rearrange("p (j d) -> p j d", d=P), bias2(wb[q]), ALU.add).then_inc(yb_sb, 1)
                dve.wait_ge(yb_sb, n + 1)
                T(yo[q], yo[q], block_rows(n)[:, :, 0:1].to_broadcast([P, 2, P]), ALU.mult).then_inc(y_sb, 1)

            with dve.Fori(0, EARLY) as s:
                add_shared(s)
            dve.wait_ge(pay_sb, NG)
            low(0, 0)
            blocks(dve, step)
            weigh(NBLK - 1, (NBLK - 1) % DEPTH)

            dve.wait_ge(sum_sb, NU)

            def sums(q):
                for r in range(QG):
                    g = q * QG + r
                    if g in POOL_SUMS:
                        dve.wait_ge(pool_total, POOL_SUMS.index(g) + 1)
                    else:
                        dve.wait_ge(ysum_sb, g + 1)
                        T(total[g], total[g], yb[g][:, :, 1, :], ALU.add).then_inc(total_sb, 1)
                        yield
                        dve.wait_ge(total_sb, sum(k not in POOL_SUMS for k in range(g + 1)))
                    for t in range(TPG):
                        ins = dve.bn_stats(st2[q % 2][:, r * TPG + t, :], total[g][:, t, :])
                        if r == QG - 1 and t == TPG - 1:
                            ins.then_inc(stats2, 1)
                        yield

            def norm_sums(q):
                v = q % 2
                dve.wait_ge(stats2, q + 1)
                yield from moments(moment2, q, st2[v], mt2, mean2, veps2)
                reused(dve, out_sb, q, 2, QG)
                yield from reciprocal_root(rsqrt2, q, veps2[:, :], rsq2, rstd2[v][:, :])
                dve.scalar_tensor_tensor(out=nbias2[v][:, :], in0=mean2[:, :], scalar=-1.0, in1=rstd2[v][:, :],
                                         op0=ALU.mult, op1=ALU.mult).then_inc(norm2, 1)

            in_turns(sums(0))
            for q in range(1, NG // QG):
                in_turns(norm_sums(q - 1), sums(q))
            in_turns(norm_sums(NG // QG - 1))
            dve.wait_ge(norm2, NG // QG)
            for g in DVE_NORMS:
                normalise(dve, g).then_inc(out_dve, 1)


_INS = ['L0_attn_u', 'L0_attn_a_params', 'L0_attn_B_w', 'L0_attn_C_w', 'L0_attn_D', 'L0_ffn_router_w', 'L0_ffn_router_b',
        'L0_ffn_sw1', 'L0_ffn_sb1', 'L0_ffn_sw2', 'L0_ffn_sb2', 'L0_ffn_rw1', 'L0_ffn_rb1', 'L0_ffn_rw2', 'L0_ffn_rb2']
_OUTS = [((NSEQ, SEQ, P), 'float32')]


def kernel(**inputs):
    import numpy as _np
    import concourse.bacc as _bacc
    from concourse import mybir as _mybir
    from concourse.bass_utils import run_bass_kernel_spmd as _run

    nc = _bacc.Bacc("TRN2", target_bir_lowering=False, num_devices=1)
    arrays, args = {}, []
    consts, pads, _ = shape_constants()
    for name, a in [("consts", consts), ("pads", pads)] + [(n, inputs[n]) for n in _INS]:
        a = _np.ascontiguousarray(a)
        arrays[f"in_{name}_dram"] = a
        args.append(nc.dram_tensor(f"in_{name}_dram", a.shape, _mybir.dt.from_np(a.dtype), kind="ExternalInput").ap())
    for i, (shape, dtype) in enumerate(_OUTS):
        dt = _mybir.dt.from_np(_np.dtype(dtype))
        args.append(nc.dram_tensor(f"out_{i}_dram", shape, dt, kind="ExternalOutput").ap())
    build(nc, *args)
    r = _run(nc, [arrays], core_ids=[0])
    got = tuple(r.results[0][f"out_{i}_dram"] for i in range(len(_OUTS)))
    return got[0]
```
